# Optimizing a Trainium2 kernel written in Bass

```python
import numpy as np
import jax
import jax.numpy as jnp

def _softmax(x, axis=-1):
    return jax.nn.softmax(x, axis=axis)

def _gelu(x):
    return jax.nn.gelu(x, approximate=True)

def _silu(x):
    return jax.nn.silu(x)

def _sigmoid(x):
    return jax.nn.sigmoid(x)

def _layernorm(x, axis=-1, eps=1e-05):
    m = jnp.mean(x, axis=axis, keepdims=True)
    v = jnp.var(x, axis=axis, keepdims=True)
    return (x - m) / jnp.sqrt(v + eps)

def _scatter_add(tgt, idx, src, axis=0):
    return tgt.at[idx].add(src)

def _segment_sum(src, seg, n):
    return jax.ops.segment_sum(src, seg, n)
kernel_name = 'mk_flamingo_gated_d1_seqx_r8_472787'

def setup_inputs(seed: int=0):
    np.random.seed(seed)
    _w = jnp.asarray

    def _rec_inputs():
        import jax
        import jax.numpy as jnp
        _rk = jax.random.key(seed)
        x = -0.0002928 + 1 * jax.random.normal(jax.random.fold_in(_rk, 1), (16, 128, 256), jnp.float32)
        _lenS = 128 - jax.random.randint(jax.random.fold_in(_rk, 7), (16,), 0, max(1, 128 // 4) + 1, jnp.int32)
        _lenS2 = 128 - jax.random.randint(jax.random.fold_in(_rk, 8), (16,), 0, max(1, 128 // 4) + 1, jnp.int32)
        fside_S2_0 = -0.00337071 + 1.01897 * jax.random.normal(jax.random.fold_in(_rk, 11), (128,), jnp.float32)
        _ctx_2048P = jax.random.normal(jax.random.fold_in(_rk, 12), (16, 16, 256), jnp.float32)
        _ctx_2048c = jax.random.dirichlet(jax.random.fold_in(_rk, 512), 0.3 * jnp.ones((16,), jnp.float32), (16, 128))
        _ctx_2048t = jnp.einsum('bsk,bkd->bsd', _ctx_2048c, _ctx_2048P)
        _ctx_2048t = _ctx_2048t * jax.lax.rsqrt(jnp.mean(jnp.square(_ctx_2048t)) + 1e-12) * 0.953939
        ctx_2048 = 0.000675642 + 1.00031 * (_ctx_2048t + 0.3 * jax.random.normal(jax.random.fold_in(_rk, 612), (16, 128, 256), jnp.float32))
        _g = jax.random.normal(jax.random.fold_in(_rk, 9001), (2, 1), jnp.float32)
        _g = jnp.sign(_g) * jnp.maximum(jnp.abs(_g), 1.0) + (_g == 0) * 1.0
        g_xattn = _g[0]
        g_ffn = _g[1]
        return (x, fside_S2_0, ctx_2048, g_xattn, g_ffn)
    x, fside_S2_0, ctx_2048, g_xattn, g_ffn = _rec_inputs()

    def _L0_xattn_setup():
        import jax, jax.numpy as jnp
        import numpy as np
        key = jax.random.key(seed)
        ks = jax.random.split(key, 5)
        B, D, L, NH = (2, 128, 256, 8)
        H = D // NH
        return {'v': jax.random.normal(ks[0], (B, D, L), jnp.float32), 'k': jax.random.normal(ks[1], (H, L), jnp.float32) * 0.1, 'bias': jax.random.normal(ks[2], (D,), jnp.float32), 'x1': jax.random.normal(ks[3], (B, D, L), jnp.float32), 'x2': jax.random.normal(ks[4], (B, D, L), jnp.float32), 'num_heads': NH}
    _L0_xattn_all = _L0_xattn_setup()
    _L0_xattn_in = {k: v for k, v in _L0_xattn_all.items() if k in ('k',)}
    del _L0_xattn_all

    def _L0_ffn_setup():
        import jax, jax.numpy as jnp
        import numpy as np
        K_TOP = 2
        key = jax.random.key(seed)
        k0, k1, k2 = jax.random.split(key, 3)
        B, S, D, E, F = (4, 256, 256, 8, 256)
        x = jax.random.normal(k0, (B, S, D), dtype=jnp.float32)
        Wr = jax.random.normal(k1, (D, E), dtype=jnp.float32) * 0.02
        We = jax.random.normal(k2, (E, D, F), dtype=jnp.float32) * 0.02
        be = jnp.zeros((E, F), dtype=jnp.float32)
        return {'x': x, 'Wr': Wr, 'We': We, 'be': be}
    _L0_ffn_all = _L0_ffn_setup()
    _L0_ffn_in = {k: v for k, v in _L0_ffn_all.items() if k in ('Wr', 'We', 'be')}
    del _L0_ffn_all
    return {'x': x, 'fside_S2_0': fside_S2_0, 'ctx_2048': ctx_2048, 'g_xattn': g_xattn, 'g_ffn': g_ffn, 'L0_xattn_k': _L0_xattn_in['k'], 'L0_ffn_Wr': _L0_ffn_in['Wr'], 'L0_ffn_We': _L0_ffn_in['We'], 'L0_ffn_be': _L0_ffn_in['be']}

def reference(x, fside_S2_0, ctx_2048, g_xattn, g_ffn, L0_xattn_k, L0_ffn_Wr, L0_ffn_We, L0_ffn_be):
    import jax
    import jax.numpy as jnp

    def _L0_xattn_ref(v, k, bias, x1, x2, num_heads):
        import jax, jax.numpy as jnp
        import numpy as np
        B, D, L = v.shape
        H = D // num_heads
        fft_size = 2 * L
        vr = v.reshape(B, H, num_heads, L)
        x1r = x1.reshape(B, H, num_heads, L)
        x2r = x2.reshape(B, H, num_heads, L)
        kv = vr[:, :, :, None, :] * x2r[:, :, None, :, :]
        k_f = jnp.fft.rfft(k.astype(jnp.float32), n=fft_size)
        y = jnp.fft.irfft(jnp.fft.rfft(kv, n=fft_size) * k_f[None, :, None, None, :], n=fft_size)[..., :L]
        skip = bias.astype(jnp.float32).reshape(H, num_heads)[None, :, :, None, None]
        y = y + kv * skip
        out = jnp.einsum('bhijl,bhil->bhjl', y, x1r)
        return out.reshape(B, D, L)

    def _L0_ffn_ref(x, Wr, We, be):
        import jax, jax.numpy as jnp
        import numpy as np
        K_TOP = 2
        logits = jnp.einsum('bsd,de->bse', x, Wr)
        w, sel = jax.lax.top_k(logits, K_TOP)
        w = jax.nn.softmax(w, axis=-1)
        E = We.shape[0]
        gate = jnp.einsum('bsk,bske->bse', w, jax.nn.one_hot(sel, E, dtype=w.dtype))
        out = jnp.zeros(x.shape[:2] + (We.shape[2],), dtype=x.dtype)
        for e in range(E):
            out = out + gate[..., e:e + 1] * (jnp.einsum('bsd,df->bsf', x, We[e]) + be[e])
        return out
    x = x + jnp.tanh(g_xattn[0]) * _L0_xattn_ref(_layernorm(x, axis=-1), L0_xattn_k, fside_S2_0, ctx_2048, ctx_2048, 8)
    x = x + jnp.tanh(g_ffn[0]) * _L0_ffn_ref(_layernorm(x, axis=-1), L0_ffn_Wr, L0_ffn_We, L0_ffn_be)
    return x

_drawn_inputs = setup_inputs


def setup_inputs(seed=0):
    import zlib

    import numpy as np

    out = dict(_drawn_inputs(seed))
    spreads = {'L0_ffn_be': (0.0, 0.459)}
    factors = {}
    for name, (base, spread) in spreads.items():
        noise = np.random.default_rng([zlib.crc32(name.encode()), seed]).standard_normal(out[name].shape)
        drawn = base * np.exp(spread * noise) if base else spread * noise
        out[name] = jnp.asarray(drawn.astype(out[name].dtype))
    for name, factor in factors.items():
        out[name] = (out[name] * factor).astype(out[name].dtype)
    return out
```

```python
import concourse.bass as bass
from concourse import mybir
from concourse.alu_op_type import AluOpType as ALU
from contextlib import ExitStack

F32 = mybir.dt.float32
F32R = mybir.dt.float32r
U32 = mybir.dt.uint32
ACT = mybir.ActivationFunctionType

P = 128
B, S, L = 16, 128, 256
H = 16
J = S // H
E, F = 8, 256
TOP = 2
EPS = 1e-5
BG = 4
G = B // BG
LB = L // P
PAIR = J * J
HALF = 2
BH = BG // HALF
QUADS = 4
QH = H // QUADS
UNITS = BG * E // 2
KPAD = P + L

V_TURN, C_TURN, SKIP_TURN, MIX_TURN, XN_TURN, TURNS = 0, 2, 4, 6, 8, 10

HEAD_UNITS = {2: 7, 5: 8, 8: 9, 11: 10, 14: 11}
WCH = 8
WCW = LB * E * F // WCH
LO_HEADS = (1, 2, 3, 4, 6, 7, 8, 10)
STATS_HEADS = 12


def build(nc, x, bias, ctx_in, g_xattn, g_ffn, toep_in, wr, we, be, out):
    es = ExitStack()
    with es:
        def sb(name, shape, dt=F32):
            return es.enter_context(nc.sbuf_tensor(name, shape, dt))

        def sem(name):
            return es.enter_context(nc.semaphore(name))

        def bank(name, shape):
            return es.enter_context(nc.psum_tensor(name, shape, F32))

        ident = sb("ident", [P, P])
        head_ones = sb("head_ones", [P, P])
        toep = sb("toep", [P, H, L])
        we_f = sb("we_f", [P, LB, E, F])
        we_hi = sb("we_hi", [P, LB, E, F], F32R)
        we_lo = sb("we_lo", [P, LB, E, F], F32R)
        wr_f = sb("wr_f", [P, LB, E])
        wr_hi = sb("wr_hi", [P, LB, E], F32R)
        wr_lo = sb("wr_lo", [P, LB, E], F32R)
        be_sb = sb("be_sb", [E, F])
        bias_sb = sb("bias_sb", [P, 1])
        bias_g = sb("bias_g", [P, 1])
        g_raw = sb("g_raw", [P, 2])
        g_tanh = sb("g_tanh", [P, 2])
        g_half = sb("g_half", [P, 2])
        eps = sb("eps", [P, 1])
        iota_e = sb("iota_e", [P, E])

        x_sb = sb("x_sb", [P, B * L])
        stats = sb("stats", [P, B, 6])
        mv = sb("mv", [P, B, 2])
        sd = sb("sd", [P, B])
        rstd = sb("rstd", [P, B])
        shift = sb("shift", [P, B])
        ctx_sb = sb("ctx_sb", [P, BG, L])
        v_sb = sb("v_sb", [P, BG, L])
        w_sb = sb("w_sb", [P, BG, L])
        t_sb = sb("t_sb", [P, BG, L])
        xt_sb = sb("xt_sb", [P, BG, L])
        vT = sb("vT", [P, LB, BG, S])
        cT = sb("cT", [P, LB, BG, S])
        kv = sb("kv", [P, 4, LB * BG, J, J])
        z_sb = sb("z_sb", [P, 2, QH, LB * BG, J, J])
        z4 = sb("z4", [P, 2, QH, LB * BG, J // 2, J])
        z2 = sb("z2", [P, QH, LB * BG, J // 4, J])
        mixT = sb("mixT", [P, LB * BG, H, J])

        x1 = sb("x1", [P, BG, L])
        stats1 = sb("stats1", [P, BG, 6])
        mv1 = sb("mv1", [P, BG, 2])
        sd1 = sb("sd1", [P, BG])
        rstd1 = sb("rstd1", [P, BG])
        xn = sb("xn", [P, BG, L])
        xnT_hi = sb("xnT_hi", [P, BG, LB, S], F32R)
        xnT_lo = sb("xnT_lo", [P, BG, LB, S], F32R)
        logits = sb("logits", [P, BG, E])
        top8 = sb("top8", [P, BG, 8])
        idx8 = sb("idx8", [P, BG, 8], U32)
        idxf = sb("idxf", [P, BG, TOP])
        diff = sb("diff", [P, BG])
        tdiff = sb("tdiff", [P, BG])
        wts = sb("wts", [P, BG, TOP])
        gk = sb("gk", [P, TOP, BG, E])
        gate = sb("gate", [P, BG, E])
        gateT = sb("gateT", [E, BG, S])
        acc = sb("acc", [P, BG, F])

        Y = [bank(f"Y{n}", [P, LB * BG, PAIR]) for n in range(2)]
        M = [bank(f"M{n}", [P, 2, F]) for n in range(2)]
        T = [bank(f"T{n}", [P, 4, P]) for n in range(2)]
        R = bank("R", [P, 512])
        Z = bank("Z", [P, BH, F])

        x_first, x_rest, ctx_s = sem("x_first"), sem("x_rest"), sem("ctx_loaded")
        toep_s = [sem(f"toep_loaded{q}") for q in range(QUADS)]
        we_in, small_in, g_in = sem("we_loaded"), sem("small_loaded"), sem("gains_loaded")
        ident0, ident_s = sem("ident_zeroed"), sem("ident_ready")
        ones0, ones1, ones_s = sem("ones_filled"), sem("ones_cut"), sem("head_ones_ready")
        iota_s, eps_s, tanh_s, gains_s = sem("iota_ready"), sem("eps_ready"), sem("tanh_ready"), sem("gains_ready")
        we_hi_s, we_lo_s = sem("we_hi_ready"), sem("we_lo_ready")
        wr_hi_s, wr_lo_s = sem("wr_hi_ready"), sem("wr_lo_ready")
        stats_s, mv_s, sd_s = sem("stats_ready"), sem("mean_var_ready"), sem("sd_ready")
        rstd_s, shift_s = sem("rstd_ready"), sem("shift_ready")
        v_s, w_s, t_s, xt_s = sem("v_ready"), sem("w_ready"), sem("bias_term_ready"), sem("xt_ready")
        turn_s = sem("turn_ready")
        vcT_s = sem("vT_cT_ready")
        kv_s, y_s, z_s = sem("kv_ready"), sem("y_ready"), sem("z_ready")
        z4_s, z2_s, mixT_s = sem("z4_ready"), sem("z2_ready"), sem("mixT_ready")
        x1_s, stats1_s, mv1_s = sem("x1_ready"), sem("stats1_ready"), sem("mean_var1_ready")
        sd1_s, rstd1_s, xn_s = sem("sd1_ready"), sem("rstd1_ready"), sem("xn_ready")
        xhi_s, xlo_s = sem("xnT_hi_ready"), sem("xnT_lo_ready")
        logit_s, lcopy_s, top_s, idx_s = sem("logits_ready"), sem("logits_copied"), sem("top_ready"), sem("index_ready")
        idxf_s, diff_s, tdiff_s, wts_s = sem("idxf_ready"), sem("diff_ready"), sem("tdiff_ready"), sem("weights_ready")
        gk_s, gate_s = sem("gate_parts_ready"), sem("gate_ready")
        gT_s, gTc_s, zb_s = sem("gateT_in_psum"), sem("gateT_ready"), sem("expert_bias_ready")
        start_s, acc_s, add_s = sem("acc_started"), sem("acc_half_added"), sem("unit_added")
        m_s = sem("unit_ready")
        out_s = [sem(f"out_stored{b}") for b in range(BG)]

        def after(eng, s, n):
            if not isinstance(n, int) or n > 0:
                eng.wait_ge(s, n)

        def apart(dve):
            dve.wait_ge(eps_s, 1)

        def is_first(g):
            return isinstance(g, int) and g == 0

        def half(t, c):
            return t[:, BH * c:BH * (c + 1)].rearrange("p b l -> p (b l)")

        def piece(t, n):
            return t[:].rearrange("p n e f -> p (n e f)")[:, WCW * n:WCW * (n + 1)]

        block = es.enter_context(nc.Block())

        @block.sync
        def _(sp):
            def load_x(b0, b1, s):
                sp.dma_start(x_sb[:, b0 * L:b1 * L].rearrange("p (b l) -> p b l", l=L),
                             x[b0:b1].rearrange("b s l -> s b l")).then_inc(s, 16)

            def load_ctx(g):
                after(sp, turn_s, TURNS * (g - 1) + C_TURN + HALF)
                after(sp, t_s, HALF * g)
                sp.dma_start(ctx_sb[:], ctx_in[bass.ds(g * BG, BG)].rearrange("b s l -> s b l")).then_inc(ctx_s, 16)

            def store(g, b):
                sp.wait_ge(add_s, UNITS * g + UNITS // BG * (b + 1))
                sp.dma_start(out[bass.ds(g * BG + b, 1)].rearrange("b s f -> (b s) f"), acc[:, b, :]).then_inc(out_s[b], 16)

            load_x(0, BG, x_first)
            load_ctx(0)
            for q in range(QUADS):
                sp.dma_start(toep[:, QH * q:QH * (q + 1), :], toep_in[:, QH * q:QH * (q + 1), :]).then_inc(toep_s[q], 16)
            for n in range(LB):
                sp.dma_start(we_f[:, n], we[:, P * n:P * (n + 1)].rearrange("e p f -> p e f")).then_inc(we_in, 16)
            load_x(BG, B, x_rest)
            load_ctx(1)
            def turn(g):
                store(g, 0)
                store(g, 1)
                load_ctx(g + 2)
                for b in range(2, BG):
                    store(g, b)
            with sp.Fori(0, G - 2) as g:
                turn(g)
            for g in range(G - 2, G):
                for b in range(BG):
                    store(g, b)
            for b in range(BG):
                sp.wait_ge(out_s[b], 16 * G)

        @block.gpsimd
        def _(pool):
            pool.memset(ident[:], 0.0).then_inc(ident0, 1)
            pool.wait_ge(ident0, 1)
            pool.affine_select(out=ident[:], in_=ident[:], compare_op=ALU.not_equal, fill=1.0, base=0,
                               pattern=[[-1, P]], channel_multiplier=1).then_inc(ident_s, 1)
            pool.memset(head_ones[:], 1.0).then_inc(ones0, 1)
            pool.wait_ge(ones0, 1)
            pool.affine_select(out=head_ones[:], in_=head_ones[:], compare_op=ALU.is_ge, fill=0.0, base=0,
                               pattern=[[-J, H], [0, J]], channel_multiplier=1).then_inc(ones1, 1)
            pool.wait_ge(ones1, 1)
            pool.affine_select(out=head_ones[:], in_=head_ones[:], compare_op=ALU.is_ge, fill=0.0, base=J - 1,
                               pattern=[[J, H], [0, J]], channel_multiplier=-1).then_inc(ones_s, 1)
            pool.iota(iota_e[:], [[1, E]], base=0, channel_multiplier=0,
                      allow_small_or_imprecise_dtypes=True).then_inc(iota_s, 1)

            def pairs(g, h):
                if h == 0:
                    pool.wait_ge(vcT_s, 4 * g + 4)
                after(pool, y_s, H * g + h - 3)
                s = slice(J * h, J * (h + 1))
                vi = vT[:, :, :, s].rearrange("p n b i -> p (n b) i").unsqueeze(3).broadcast_to([P, LB * BG, J, J])
                cj = cT[:, :, :, s].rearrange("p n b i -> p (n b) i").unsqueeze(2).broadcast_to([P, LB * BG, J, J])
                pool.tensor_tensor(kv[:, h % 4], vi, cj, ALU.mult).then_inc(kv_s, 1)

            def halve(g, q):
                pool.wait_ge(z_s, H * g + QH * (q + 1))
                after(pool, z2_s, QUADS * g + q - 1)
                z = z_sb[:, q % 2].rearrange("p h n i j -> p (h n) (i j)")
                o = z4[:, q % 2].rearrange("p h n i j -> p (h n) (i j)")
                pool.tensor_tensor(o, z[:, :, 0:PAIR // 2], z[:, :, PAIR // 2:], ALU.add).then_inc(z4_s, 1)

            def add_bias_term(g, c):
                pool.wait_ge(t_s, HALF * g + c + 1)
                after(pool, x1_s, HALF * g)
                pool.tensor_tensor(half(xt_sb, c), x_sb[:, bass.ds((g * BG + BH * c) * L, BH * L)],
                                   half(t_sb, c), ALU.add).then_inc(xt_s, 1)

            def group(g):
                for h in range(H):
                    pairs(g, h)
                    if h >= QH + 1 and h % QH == 1:
                        halve(g, h // QH - 1)
                    if h in (2, 3):
                        add_bias_term(g, h - 2)
                    if is_first(g) and h in LO_HEADS:
                        n = LO_HEADS.index(h)
                        pool.wait_ge(we_hi_s, n + 1)
                        pool.tensor_tensor(piece(we_lo, n), piece(we_f, n), piece(we_hi, n), ALU.subtract).then_inc(we_lo_s, 1)
                halve(g, QUADS - 1)

            group(0)
            with pool.Fori(1, G) as g:
                group(g)

        @block.scalar
        def _(act):
            act.dma_start(g_raw[:, 0:1], g_xattn.partition_broadcast(P)).then_inc(g_in, 16)
            act.dma_start(g_raw[:, 1:2], g_ffn.partition_broadcast(P)).then_inc(g_in, 16)
            act.dma_start(bias_sb[:], bias.rearrange("(s o) -> s o", o=1)).then_inc(g_in, 16)
            act.dma_start(wr_f[:], wr.rearrange("(n p) e -> p n e", p=P)).then_inc(small_in, 16)
            act.dma_start(be_sb[:], be).then_inc(small_in, 16)
            act.wait_ge(g_in, 48)
            act.activation(g_tanh[:], g_raw[:], ACT.Tanh).then_inc(tanh_s, 1)

            def root(b0, b1):
                act.wait_ge(eps_s, 1)
                act.wait_ge(mv_s, b1)
                act.activation(sd[:, b0:b1], mv[:, b0:b1, 1], ACT.Sqrt, bias=eps[:]).then_inc(sd_s, 1)

            def normalise(g):
                if is_first(g):
                    act.wait_ge(shift_s, 1)
                else:
                    act.wait_ge(shift_s, 2)
                    act.wait_ge(turn_s, TURNS * (g - 1) + V_TURN + HALF)
                    act.wait_ge(w_s, HALF * g)
                for b in range(BG):
                    n = g * BG + b
                    act.activation(v_sb[:, b], x_sb[:, bass.ds(n * L, L)], ACT.Identity,
                                   bias=shift[:, bass.ds(n, 1)], scale=rstd[:, bass.ds(n, 1)]).then_inc(v_s, 1)

            def keep(g, turn, dst, c):
                act.wait_ge(turn_s, TURNS * g + turn + c + 1)
                act.activation(dst[:, :, BH * c:BH * (c + 1), :],
                               T[(turn + c) % 2][:].rearrange("p (n b) s -> p n b s", n=LB), ACT.Copy).then_inc(vcT_s, 1)

            def root1(g, c):
                o = slice(BH * c, BH * (c + 1))
                act.wait_ge(mv1_s, BG * g + BH * (c + 1))
                act.activation(sd1[:, o], mv1[:, o, 1], ACT.Sqrt, bias=eps[:]).then_inc(sd1_s, 1)

            def round_xn(g, c):
                act.wait_ge(turn_s, TURNS * g + XN_TURN + c + 1)
                after(act, m_s, UNITS * (g - 1) + UNITS // HALF * (c + 1))
                act.activation(xnT_hi[:, BH * c:BH * (c + 1)].rearrange("p b n s -> p (b n) s"), T[(XN_TURN + c) % 2][:],
                               ACT.Copy).then_inc(xhi_s, 1)

            def group(g):
                normalise(g)
                for turn, dst in ((V_TURN, vT), (C_TURN, cT)):
                    for c in range(HALF):
                        keep(g, turn, dst, c)
                if is_first(g):
                    act.wait_ge(we_in, 16 * LB)
                    for n in range(WCH):
                        act.activation(piece(we_hi, n), piece(we_f, n), ACT.Copy).then_inc(we_hi_s, 1)
                    act.wait_ge(small_in, 32)
                    act.activation(wr_hi[:], wr_f[:], ACT.Copy).then_inc(wr_hi_s, 1)
                    root(BG, B)
                root1(g, 0)
                root1(g, 1)
                round_xn(g, 0)
                round_xn(g, 1)
                act.wait_ge(diff_s, g + 1)
                act.activation(tdiff[:], diff[:], ACT.Tanh, scale=0.5).then_inc(tdiff_s, 1)
                act.wait_ge(gT_s, g + 1)
                act.activation(gateT[:], R[0:E, :].rearrange("e (b s) -> e b s", b=BG), ACT.Copy).then_inc(gTc_s, 1)

            root(0, BG)
            group(0)
            with act.Fori(1, G) as g:
                group(g)

        @block.tensor
        def _(pe):
            pe.wait_ge(ident_s, 1)

            def turn4(turn, blocks):
                for n, block_ in enumerate(blocks):
                    last = pe.transpose(T[turn % 2][:, n, :], block_, ident[:])
                last.then_inc(turn_s, 1)

            def transpose_v(g, c):
                pe.wait_ge(v_s, BG * g + BH * (c + 1))
                after(pe, xlo_s, HALF * (g - 1) + c + 1)
                turn4(V_TURN + c, [v_sb[:, b, P * n:P * (n + 1)] for n in range(LB) for b in range(BH * c, BH * (c + 1))])

            def transpose_c(g, c):
                pe.wait_ge(ctx_s, 16 * (g + 1))
                pe.wait_ge(vcT_s, 4 * g + c + 1)
                turn4(C_TURN + c, [ctx_sb[:, b, P * n:P * (n + 1)] for n in range(LB) for b in range(BH * c, BH * (c + 1))])

            def sum_heads(g, c):
                if is_first(g):
                    pe.wait_ge(ones_s, 1)
                pe.wait_ge(w_s, HALF * g + c + 1)
                pe.wait_ge(vcT_s, 4 * g + HALF + c + 1)
                pe.matmul(T[(SKIP_TURN + c) % 2][:].rearrange("p n s -> p (n s)"), head_ones[:], half(w_sb, c),
                          start=True, stop=True).then_inc(turn_s, 1)

            def conv(g, h):
                if is_first(g) and h % QH == 0:
                    pe.wait_ge(toep_s[h // QH], 16)
                pe.wait_ge(kv_s, H * g + h + 1)
                after(pe, z_s, H * g + h - 1)
                y = Y[h % 2][:].rearrange("p n q -> p (n q)")
                m = kv[:, h % 4].rearrange("p n i j -> p (n i j)")
                lower = BG * PAIR
                pe.matmul(y, toep[:, h, 0:P], m, start=True, stop=False)
                pe.matmul(y[:, lower:], toep[:, h, P:L], m[:, 0:lower], start=False, stop=True).then_inc(y_s, 1)

            def unit(g, u):
                b, e = u // (E // 2), 2 * (u % (E // 2))
                if is_first(g) and u == 0:
                    pe.wait_ge(we_lo_s, WCH)
                after(pe, add_s, UNITS * g + u - 1)
                o = M[u % 2][:]
                for n in range(LB):
                    pe.matmul(o, xnT_hi[:, b, n], we_hi[:, n, e:e + 2], start=(n == 0), stop=False)
                    pe.matmul(o, xnT_hi[:, b, n], we_lo[:, n, e:e + 2], start=False, stop=False)
                    last = pe.matmul(o, xnT_lo[:, b, n], we_hi[:, n, e:e + 2], start=False, stop=(n == LB - 1))
                last.then_inc(m_s, 1)

            def transpose_mix(g, c):
                pe.wait_ge(mixT_s, QUADS * (g + 1))
                pe.wait_ge(t_s, HALF * g + c + 1)
                turn4(MIX_TURN + c, [mixT[:, n * BG + b].rearrange("p h j -> p (h j)")
                                     for b in range(BH * c, BH * (c + 1)) for n in range(LB)])

            def transpose_xn(g, c):
                pe.wait_ge(xn_s, BG * g + BH * (c + 1))
                pe.wait_ge(x1_s, HALF * g + c + 1)
                turn4(XN_TURN + c, [xn[:, b, P * n:P * (n + 1)] for b in range(BH * c, BH * (c + 1)) for n in range(LB)])

            def route(g):
                if is_first(g):
                    pe.wait_ge(wr_lo_s, 1)
                pe.wait_ge(xlo_s, HALF * (g + 1))
                after(pe, gTc_s, g)
                for b in range(BG):
                    terms = [(x_, w_, n) for n in range(LB) for x_ in (xnT_hi, xnT_lo) for w_ in (wr_hi, wr_lo)]
                    for t, (x_, w_, n) in enumerate(terms):
                        last = pe.matmul(R[:, E * b:E * (b + 1)], x_[:, b, n], w_[:, n], start=(t == 0), stop=(t == len(terms) - 1))
                last.then_inc(logit_s, 1)

            def transpose_gates(g):
                pe.wait_ge(gate_s, g + 1)
                for b in range(BG):
                    last = pe.matmul(R[0:E, S * b:S * (b + 1)], gate[:, b], ident[:], start=True, stop=True)
                last.then_inc(gT_s, 1)

            def expert_bias(g, c):
                if is_first(g):
                    pe.wait_ge(small_in, 32)
                pe.wait_ge(gTc_s, g + 1)
                after(pe, start_s, HALF * g + c)
                for b in range(BH):
                    last = pe.matmul(Z[:, b], gateT[:, BH * c + b], be_sb[:], start=True, stop=True)
                last.then_inc(zb_s, 1)

            def group(g):
                def before(u):
                    if not is_first(g):
                        unit(g - 1, u)

                before(4)
                transpose_v(g, 0)
                transpose_v(g, 1)
                before(5)
                transpose_c(g, 0)
                transpose_c(g, 1)
                before(6)
                sum_heads(g, 0)
                sum_heads(g, 1)
                for h in range(H):
                    conv(g, h)
                    if h in HEAD_UNITS:
                        before(HEAD_UNITS[h])
                before(12)
                transpose_mix(g, 0)
                transpose_mix(g, 1)
                before(13)
                before(14)
                transpose_xn(g, 0)
                before(15)
                transpose_xn(g, 1)
                route(g)
                unit(g, 0)
                unit(g, 1)
                transpose_gates(g)
                expert_bias(g, 0)
                unit(g, 2)
                expert_bias(g, 1)
                unit(g, 3)

            group(0)
            with pe.Fori(1, G) as g:
                group(g)
            for u in range(4, UNITS):
                unit(G - 1, u)

        @block.vector
        def _(dve):
            dve.memset(eps[:], EPS).then_inc(eps_s, 1)

            def row_stats(b):
                dve.bn_stats(stats[:, b], x_sb[:, L * b:L * (b + 1)]).then_inc(stats_s, 1)
                dve.wait_ge(stats_s, b + 1)
                dve.bn_aggr(mv[:, b], stats[:, b]).then_inc(mv_s, 1)

            def scales(b0, b1, n):
                dve.wait_ge(sd_s, n)
                dve.reciprocal(rstd[:, b0:b1], sd[:, b0:b1]).then_inc(rstd_s, 1)
                dve.wait_ge(rstd_s, n)
                dve.scalar_tensor_tensor(out=shift[:, b0:b1], in0=mv[:, b0:b1, 0], scalar=-1.0, in1=rstd[:, b0:b1],
                                         op0=ALU.mult, op1=ALU.mult).then_inc(shift_s, 1)

            def products(g, c):
                dve.wait_ge(ctx_s, 16 * (g + 1))
                dve.wait_ge(v_s, BG * g + BH * (c + 1))
                after(dve, turn_s, TURNS * (g - 1) + SKIP_TURN + c + 1)
                dve.scalar_tensor_tensor(out=half(w_sb, c), in0=half(v_sb, c), scalar=bias_g[:], in1=half(ctx_sb, c),
                                         op0=ALU.mult, op1=ALU.mult).then_inc(w_s, 1)

            def bias_term(g, c):
                dve.wait_ge(turn_s, TURNS * g + SKIP_TURN + c + 1)
                after(dve, xt_s, HALF * (g - 1) + c + 1)
                dve.tensor_tensor(half(t_sb, c), T[(SKIP_TURN + c) % 2][:].rearrange("p n s -> p (n s)"),
                                  half(ctx_sb, c), ALU.mult).then_inc(t_s, 1)

            def weigh(g, h):
                dve.wait_ge(y_s, H * g + h + 1)
                q = h // QH
                if h % QH == 0:
                    after(dve, z4_s, QUADS * g + q - 1)
                ci = cT[:, :, :, J * h:J * (h + 1)].rearrange("p n b i -> p (n b) i").unsqueeze(3)
                dve.tensor_tensor(z_sb[:, q % 2, h % QH], Y[h % 2][:].rearrange("p n (i j) -> p n i j", i=J),
                                  ci.broadcast_to([P, LB * BG, J, J]), ALU.mult).then_inc(z_s, 1)

            def reduce(g, q):
                dve.wait_ge(z4_s, QUADS * g + q + 1)
                after(dve, mixT_s, QUADS * g + q)
                z = z4[:, q % 2].rearrange("p h n i j -> p (h n) (i j)")
                dve.tensor_tensor(z2[:].rearrange("p h n i j -> p (h n) (i j)"), z[:, :, 0:2 * J], z[:, :, 2 * J:],
                                  ALU.add).then_inc(z2_s, 1)
                dve.wait_ge(z2_s, QUADS * g + q + 1)
                if q == 0:
                    after(dve, turn_s, TURNS * (g - 1) + MIX_TURN + HALF)
                a, b = (z2[:, :, :, i].rearrange("p h n j -> p n h j") for i in range(2))
                dve.tensor_tensor(mixT[:, :, QH * q:QH * (q + 1)], a, b, ALU.add).then_inc(mixT_s, 1)

            def residual(g, c):
                dve.wait_ge(turn_s, TURNS * g + MIX_TURN + c + 1)
                dve.wait_ge(xt_s, HALF * g + c + 1)
                after(dve, start_s, HALF * g)
                dve.scalar_tensor_tensor(out=half(x1, c), in0=T[(MIX_TURN + c) % 2][:].rearrange("p n s -> p (n s)"),
                                         scalar=g_tanh[:, 0:1], in1=half(xt_sb, c), op0=ALU.mult, op1=ALU.add).then_inc(x1_s, 1)

            def row_stats1(g, c):
                dve.wait_ge(x1_s, HALF * g + c + 1)
                for b in range(BH * c, BH * (c + 1)):
                    dve.bn_stats(stats1[:, b], x1[:, b]).then_inc(stats1_s, 1)
                for b in range(BH * c, BH * (c + 1)):
                    apart(dve)
                    dve.wait_ge(stats1_s, BG * g + b + 1)
                    dve.bn_aggr(mv1[:, b], stats1[:, b]).then_inc(mv1_s, 1)

            def normalise1(g, c):
                o = slice(BH * c, BH * (c + 1))
                dve.wait_ge(sd1_s, HALF * g + c + 1)
                dve.reciprocal(rstd1[:, o], sd1[:, o]).then_inc(rstd1_s, 1)
                dve.wait_ge(rstd1_s, HALF * g + c + 1)
                after(dve, turn_s, TURNS * (g - 1) + XN_TURN + c + 1)
                for b in range(BH * c, BH * (c + 1)):
                    dve.tensor_scalar(xn[:, b], x1[:, b], mv1[:, b, 0:1], rstd1[:, b:b + 1],
                                      ALU.subtract, ALU.mult).then_inc(xn_s, 1)

            def rest_xn(g, c):
                dve.wait_ge(xhi_s, HALF * g + c + 1)
                o = slice(BH * c, BH * (c + 1))
                dve.tensor_tensor(xnT_lo[:, o].rearrange("p b n s -> p (b n) s"), T[(XN_TURN + c) % 2][:],
                                  xnT_hi[:, o].rearrange("p b n s -> p (b n) s"), ALU.subtract).then_inc(xlo_s, 1)

            def gates(g):
                dve.wait_ge(logit_s, g + 1)
                dve.tensor_copy(logits[:], R[:, 0:BG * E].rearrange("p (b e) -> p b e", b=BG)).then_inc(lcopy_s, 1)
                apart(dve)
                dve.wait_ge(lcopy_s, g + 1)
                for b in range(BG):
                    dve.max(top8[:, b], logits[:, b]).then_inc(top_s, 1)
                for b in range(BG):
                    apart(dve)
                    dve.wait_ge(top_s, BG * g + b + 1)
                    dve.max_index(idx8[:, b], top8[:, b], logits[:, b]).then_inc(idx_s, 1)
                dve.tensor_tensor(diff[:], top8[:, :, 0], top8[:, :, 1], ALU.subtract).then_inc(diff_s, 1)
                dve.wait_ge(idx_s, BG * (g + 1))
                dve.tensor_copy(idxf[:], idx8[:, :, 0:TOP]).then_inc(idxf_s, 1)
                dve.wait_ge(tdiff_s, g + 1)
                for k in range(TOP):
                    dve.tensor_scalar(wts[:, :, k], tdiff[:], g_half[:, k:k + 1], g_half[:, 0:1], ALU.mult, ALU.add).then_inc(wts_s, 1)
                dve.wait_ge(idxf_s, g + 1)
                dve.wait_ge(wts_s, TOP * (g + 1))
                for b in range(BG):
                    for k in range(TOP):
                        dve.tensor_scalar(gk[:, k, b], iota_e[:], idxf[:, b, k:k + 1], wts[:, b, k:k + 1],
                                          ALU.is_equal, ALU.mult).then_inc(gk_s, 1)
                dve.wait_ge(gk_s, BG * TOP * (g + 1))
                after(dve, add_s, UNITS * g)
                dve.tensor_tensor(gate[:], gk[:, 0], gk[:, 1], ALU.add).then_inc(gate_s, 1)

            def start(g, c):
                dve.wait_ge(zb_s, HALF * g + c + 1)
                for b in range(BH * c, BH * (c + 1)):
                    after(dve, out_s[b], 16 * g)
                dve.tensor_tensor(half(acc, c), Z[:].rearrange("p b f -> p (b f)"), half(x1, c), ALU.add).then_inc(start_s, 1)

            def add(g, u):
                b, e = u // (E // 2), 2 * (u % (E // 2))
                dve.wait_ge(m_s, UNITS * g + u + 1)
                dve.wait_ge(start_s, HALF * g + u // (UNITS // HALF) + 1)
                after(dve, add_s, UNITS * g + u)
                dve.scalar_tensor_tensor(out=acc[:, b], in0=M[u % 2][:, 0], scalar=gate[:, b, e:e + 1], in1=acc[:, b],
                                         op0=ALU.mult, op1=ALU.add).then_inc(acc_s, 1)
                dve.wait_ge(acc_s, UNITS * g + u + 1)
                dve.scalar_tensor_tensor(out=acc[:, b], in0=M[u % 2][:, 1], scalar=gate[:, b, e + 1:e + 2], in1=acc[:, b],
                                         op0=ALU.mult, op1=ALU.add).then_inc(add_s, 1)

            def group(g):
                def before(u):
                    if not is_first(g):
                        add(g - 1, u)

                before(4)
                products(g, 0)
                products(g, 1)
                before(5)
                before(6)
                bias_term(g, 0)
                bias_term(g, 1)
                for h in range(H):
                    weigh(g, h)
                    if h >= QH + 2 and h % QH == 2:
                        reduce(g, h // QH - 1)
                    if h in HEAD_UNITS:
                        before(HEAD_UNITS[h])
                    if is_first(g) and h == 0:
                        dve.wait_ge(x_rest, 16)
                    if is_first(g) and h < B - BG:
                        row_stats(BG + h)
                    if is_first(g) and h == B - BG + 1:
                        scales(BG, B, 2)
                        dve.wait_ge(wr_hi_s, 1)
                        dve.tensor_tensor(wr_lo[:], wr_f[:], wr_hi[:], ALU.subtract).then_inc(wr_lo_s, 1)
                before(12)
                reduce(g, QUADS - 1)
                for c in range(HALF):
                    residual(g, c)
                for c in range(HALF):
                    row_stats1(g, c)
                before(13)
                before(14)
                normalise1(g, 0)
                normalise1(g, 1)
                before(15)
                rest_xn(g, 0)
                rest_xn(g, 1)
                gates(g)
                start(g, 0)
                add(g, 0)
                add(g, 1)
                start(g, 1)
                add(g, 2)
                add(g, 3)

            dve.wait_ge(x_first, 16)
            for b in range(BG):
                row_stats(b)
            dve.wait_ge(tanh_s, 1)
            dve.tensor_tensor(bias_g[:], bias_sb[:], g_tanh[:, 0:1], ALU.mult).then_inc(gains_s, 1)
            for k, sign in enumerate((0.5, -0.5)):
                dve.tensor_scalar(g_half[:, k:k + 1], g_tanh[:, 1:2], sign, None, ALU.mult).then_inc(gains_s, 1)
            scales(0, BG, 1)
            dve.wait_ge(gains_s, 3)
            dve.wait_ge(iota_s, 1)
            group(0)
            with dve.Fori(1, G) as g:
                group(g)
            for u in range(4, UNITS):
                add(G - 1, u)


def kernel(x, fside_S2_0, ctx_2048, g_xattn, g_ffn, L0_xattn_k, L0_ffn_Wr, L0_ffn_We, L0_ffn_be):
    import numpy as np
    import concourse.bacc as bacc
    from concourse.bass_utils import run_bass_kernel_spmd

    kpad = np.zeros((H, KPAD), np.float32)
    kpad[:, P:] = np.asarray(L0_xattn_k)
    toep = np.lib.stride_tricks.sliding_window_view(kpad, L, axis=1)[:, P:0:-1].transpose(1, 0, 2)
    arrays = {"x": x, "bias": fside_S2_0, "ctx": ctx_2048, "g_xattn": g_xattn, "g_ffn": g_ffn, "toep": toep,
              "wr": L0_ffn_Wr, "we": L0_ffn_We, "be": L0_ffn_be}
    arrays = {f"in_{n}": np.ascontiguousarray(a) for n, a in arrays.items()}
    nc = bacc.Bacc("TRN2", target_bir_lowering=False, num_devices=1)
    args = [nc.dram_tensor(n, a.shape, mybir.dt.from_np(a.dtype), kind="ExternalInput").ap() for n, a in arrays.items()]
    out = nc.dram_tensor("out_0", (B, S, F), F32, kind="ExternalOutput").ap()
    build(nc, *args, out)
    r = run_bass_kernel_spmd(nc, [arrays], core_ids=[0])
    return r.results[0]["out_0"]
```

```python
import concourse.bass as bass
from concourse import mybir
from concourse.alu_op_type import AluOpType as ALU
from contextlib import ExitStack

F32 = mybir.dt.float32
F32R = mybir.dt.float32r
U32 = mybir.dt.uint32
ACT = mybir.ActivationFunctionType

P = 128
B, S, L = 16, 128, 256
H = 16
J = S // H
E, F = 8, 256
TOP = 2
EPS = 1e-5
BG = 4
G = B // BG
LB = L // P
PAIR = J * J
HALF = 2
BH = BG // HALF
QUADS = 4
QH = H // QUADS
UNITS = BG * E // 2
KPAD = P + L

LAG = 17
SLOTS = H + LAG + G * UNITS
KVS = 8
WCH = 8
WCW = LB * E * F // WCH


def due(slot, at, later=0):
    g, h = divmod(slot - later, H)
    return (g + at[1],) if slot >= later and h == at[0] and 0 <= g + at[1] < G else ()


def unit_at(slot):
    k = slot - H - LAG
    return (divmod(k, UNITS),) if 0 <= k < G * UNITS else ()


AT_STATS, AT_ROOT, AT_SCALES, AT_NORM = (0, 1), (4, 1), (6, 1), (6, 1)
AT_PRODUCTS, AT_V, AT_C, AT_SKIP, AT_TERM, AT_XT = (9, 1), (11, 1), (13, 1), (14, 1), (14, 1), (10, 0)
HALVE_LATER, REDUCE_LATER = 7, 6
AT_MIX, AT_RESIDUAL, AT_ROOT1, AT_NORM1 = (4, -1), (4, -1), (5, -1), (7, -1)
AT_XN, AT_ROUND, AT_REST = (9, -1), (9, -1), (9, -1)
AT_ROUTE, AT_TOP, AT_GATES = (12, -1), (12, -1), (13, -1)
AT_GATES_T, AT_BIAS0, AT_START0, AT_BIAS1, AT_START1 = (15, -1), (0, -2), (1, -2), (2, -2), (2, -2)


def due(slot, at, later=0):
    g, h = divmod(slot - later, H)
    return (g + at[1],) if slot >= later and h == at[0] and 0 <= g + at[1] < G else ()


def unit_at(slot):
    k = slot - H - LAG
    return (divmod(k, UNITS),) if 0 <= k < G * UNITS else ()


V, C, SKIP, MIX, XN = "v", "ctx", "skip", "mix", "xn"
TURNS = [(V, 0), (C, 0), (SKIP, 0)]
for _slot in range(SLOTS):
    for _kind, _at in ((MIX, AT_MIX), (XN, AT_XN), (V, AT_V), (C, AT_C), (SKIP, AT_SKIP)):
        TURNS += [(_kind, _g) for _g in due(_slot, _at)]


def turn_count(kind, g, c):
    return HALF * TURNS.index((kind, g)) + c + 1


def build(nc, x, bias, ctx_in, g_xattn, g_ffn, toep_in, wr, we, be, out):
    es = ExitStack()
    with es:
        def sb(name, shape, dt=F32):
            return es.enter_context(nc.sbuf_tensor(name, shape, dt))

        def sem(name):
            return es.enter_context(nc.semaphore(name))

        def bank(name, shape):
            return es.enter_context(nc.psum_tensor(name, shape, F32))

        ident = sb("ident", [P, P])
        head_ones = sb("head_ones", [P, P])
        toep = sb("toep", [P, H, L])
        we_f = sb("we_f", [P, LB, E, F])
        we_hi = sb("we_hi", [P, LB, E, F], F32R)
        we_lo = sb("we_lo", [P, LB, E, F], F32R)
        wr_f = sb("wr_f", [P, LB, E])
        wr_hi = sb("wr_hi", [P, LB, E], F32R)
        wr_lo = sb("wr_lo", [P, LB, E], F32R)
        be_sb = sb("be_sb", [E, F])
        bias_sb = sb("bias_sb", [P, 1])
        bias_g = sb("bias_g", [P, 1])
        g_raw = sb("g_raw", [P, 2])
        g_tanh = sb("g_tanh", [P, 2])
        g_half = sb("g_half", [P, 2])
        eps = sb("eps", [P, 1])
        iota_e = sb("iota_e", [P, E])

        x_sb = sb("x_sb", [P, B * L])
        stats = sb("stats", [P, B, 6])
        mv = sb("mv", [P, B, 2])
        sd = sb("sd", [P, B])
        rstd = sb("rstd", [P, B])
        shift = sb("shift", [P, B])
        ctx_sb = sb("ctx_sb", [P, BG, L])
        v_sb = sb("v_sb", [P, BG, L])
        w_sb = sb("w_sb", [P, BG, L])
        t_sb = sb("t_sb", [P, BG, L])
        xt_sb = sb("xt_sb", [P, BG, L])
        vT = sb("vT", [P, 2, LB, BG, S])
        cT = sb("cT", [P, 2, LB, BG, S])
        kv = sb("kv", [P, KVS, LB * BG, J, J])
        z_sb = sb("z_sb", [P, 2, QH, LB * BG, J, J])
        z4 = sb("z4", [P, 2, QH, LB * BG, J // 2, J])
        z2 = sb("z2", [P, QH, LB * BG, J // 4, J])
        mixT = sb("mixT", [P, LB * BG, H, J])

        x1 = sb("x1", [P, BG, L])
        stats1 = sb("stats1", [P, BG, 6])
        mv1 = sb("mv1", [P, BG, 2])
        sd1 = sb("sd1", [P, BG])
        rstd1 = sb("rstd1", [P, BG])
        xn = sb("xn", [P, BG, L])
        xnT_hi = sb("xnT_hi", [P, 2, BG, LB, S], F32R)
        xnT_lo = sb("xnT_lo", [P, 2, BG, LB, S], F32R)
        logits = sb("logits", [P, BG, E])
        top8 = sb("top8", [P, BG, 8])
        idx8 = sb("idx8", [P, BG, 8], U32)
        idxf = sb("idxf", [P, BG, TOP])
        diff = sb("diff", [P, BG])
        tdiff = sb("tdiff", [P, BG])
        wts = sb("wts", [P, BG, TOP])
        gk = sb("gk", [P, TOP, BG, E])
        gate = sb("gate", [P, 2, BG, E])
        gateT = sb("gateT", [E, BG, S])
        acc = sb("acc", [P, 2, BG, F])

        Y = [bank(f"Y{n}", [P, LB * BG, PAIR]) for n in range(3)]
        M = [bank(f"M{n}", [P, 2, F]) for n in range(2)]
        T = [bank(f"T{n}", [P, 4, P]) for n in range(2)]
        R = bank("R", [P, 512])

        x_in, ctx_s = [sem(f"x_loaded{g}") for g in range(G)], sem("ctx_loaded")
        toep_s = [sem(f"toep_loaded{q}") for q in range(QUADS)]
        we_in, small_in, g_in = sem("we_loaded"), sem("small_loaded"), sem("gains_loaded")
        ident0, ident_s = sem("ident_zeroed"), sem("ident_ready")
        ones0, ones1, ones_s = sem("ones_filled"), sem("ones_cut"), sem("head_ones_ready")
        iota_s, eps_s, tanh_s, gains_s = sem("iota_ready"), sem("eps_ready"), sem("tanh_ready"), sem("gains_ready")
        we_hi_s, we_lo_s = sem("we_hi_ready"), sem("we_lo_ready")
        wr_hi_s, wr_lo_s = sem("wr_hi_ready"), sem("wr_lo_ready")
        stats_s, mv_s, sd_s = sem("stats_ready"), sem("mean_var_ready"), sem("sd_ready")
        rstd_s, shift_s = sem("rstd_ready"), sem("shift_ready")
        v_s, w_s, t_s, xt_s = sem("v_ready"), sem("w_ready"), sem("bias_term_ready"), sem("xt_ready")
        turn_s = sem("turn_ready")
        vcT_s = sem("vT_cT_ready")
        kv_s, y_s, z_s = sem("kv_ready"), sem("y_ready"), sem("z_ready")
        z4_s, z2_s, mixT_s = sem("z4_ready"), sem("z2_ready"), sem("mixT_ready")
        x1_s, stats1_s, mv1_s = sem("x1_ready"), sem("stats1_ready"), sem("mean_var1_ready")
        sd1_s, rstd1_s, xn_s = sem("sd1_ready"), sem("rstd1_ready"), sem("xn_ready")
        xhi_s, xlo_s = sem("xnT_hi_ready"), sem("xnT_lo_ready")
        logit_s, lcopy_s, top_s, idx_s = sem("logits_ready"), sem("logits_copied"), sem("top_ready"), sem("index_ready")
        idxf_s, diff_s, tdiff_s, wts_s = sem("idxf_ready"), sem("diff_ready"), sem("tdiff_ready"), sem("weights_ready")
        gk_s, gate_s = sem("gate_parts_ready"), sem("gate_ready")
        gT_s, gTc_s, zb_s = sem("gateT_in_psum"), sem("gateT_ready"), sem("expert_bias_ready")
        start_s, acc_s, add_s = sem("acc_started"), sem("acc_half_added"), sem("unit_added")
        m_s = sem("unit_ready")
        out_s = [[sem(f"out_stored{n}_{b}") for b in range(BG)] for n in range(2)]

        def after(eng, s, n):
            if n > 0:
                eng.wait_ge(s, n)

        def half(t, c):
            return t[:, BH * c:BH * (c + 1)].rearrange("p b l -> p (b l)")

        def piece(t, n):
            return t[:].rearrange("p n e f -> p (n e f)")[:, WCW * n:WCW * (n + 1)]

        block = es.enter_context(nc.Block())

        @block.sync
        def _(sp):
            def load_x(g):
                sp.dma_start(x_sb[:, g * BG * L:(g + 1) * BG * L].rearrange("p (b l) -> p b l", l=L),
                             x[g * BG:(g + 1) * BG].rearrange("b s l -> s b l")).then_inc(x_in[g], 16)

            def load_ctx(g):
                after(sp, t_s, HALF * g)
                sp.dma_start(ctx_sb[:], ctx_in[g * BG:(g + 1) * BG].rearrange("b s l -> s b l")).then_inc(ctx_s, 16)

            def load_toep(q):
                sp.dma_start(toep[:, QH * q:QH * (q + 1), :], toep_in[:, QH * q:QH * (q + 1), :]).then_inc(toep_s[q], 16)

            load_x(0)
            load_ctx(0)
            load_toep(0)
            load_toep(1)
            load_x(1)
            load_toep(2)
            load_toep(3)
            for n in range(LB):
                sp.dma_start(we_f[:, n], we[:, P * n:P * (n + 1)].rearrange("e p f -> p e f")).then_inc(we_in, 16)
            for g in range(2, G):
                load_x(g)
            load_ctx(1)
            for slot in range(SLOTS):
                for g in due(slot, AT_TERM, 2):
                    if g + 1 < G:
                        load_ctx(g + 1)
                for g, u in unit_at(slot):
                    if u % (UNITS // BG) == UNITS // BG - 1:
                        b = u // (UNITS // BG)
                        sp.wait_ge(add_s, UNITS * g + u + 1)
                        sp.dma_start(out[g * BG + b], acc[:, g % 2, b, :]).then_inc(out_s[g % 2][b], 16)
            for g in (G - 2, G - 1):
                for b in range(BG):
                    sp.wait_ge(out_s[g % 2][b], 16 * (g // 2 + 1))

        @block.gpsimd
        def _(pool):
            pool.memset(ident[:], 0.0).then_inc(ident0, 1)
            pool.wait_ge(ident0, 1)
            pool.affine_select(out=ident[:], in_=ident[:], compare_op=ALU.not_equal, fill=1.0, base=0,
                               pattern=[[-1, P]], channel_multiplier=1).then_inc(ident_s, 1)
            pool.memset(head_ones[:], 1.0).then_inc(ones0, 1)
            pool.wait_ge(ones0, 1)
            pool.affine_select(out=head_ones[:], in_=head_ones[:], compare_op=ALU.is_ge, fill=0.0, base=0,
                               pattern=[[-J, H], [0, J]], channel_multiplier=1).then_inc(ones1, 1)
            pool.wait_ge(ones1, 1)
            pool.affine_select(out=head_ones[:], in_=head_ones[:], compare_op=ALU.is_ge, fill=0.0, base=J - 1,
                               pattern=[[J, H], [0, J]], channel_multiplier=-1).then_inc(ones_s, 1)
            pool.iota(iota_e[:], [[1, E]], base=0, channel_multiplier=0,
                      allow_small_or_imprecise_dtypes=True).then_inc(iota_s, 1)

            def pairs(g, h):
                if h == 0:
                    pool.wait_ge(vcT_s, 4 * g + 4)
                after(pool, y_s, H * g + h - KVS + 1)
                s = slice(J * h, J * (h + 1))
                vi = vT[:, g % 2, :, :, s].rearrange("p n b i -> p (n b) i").unsqueeze(3).broadcast_to([P, LB * BG, J, J])
                cj = cT[:, g % 2, :, :, s].rearrange("p n b i -> p (n b) i").unsqueeze(2).broadcast_to([P, LB * BG, J, J])
                pool.tensor_tensor(kv[:, h % KVS], vi, cj, ALU.mult).then_inc(kv_s, 1)

            def halve(g, q):
                pool.wait_ge(z_s, H * g + QH * (q + 1))
                after(pool, z2_s, QUADS * g + q - 1)
                z = z_sb[:, q % 2].rearrange("p h n i j -> p (h n) (i j)")
                o = z4[:, q % 2].rearrange("p h n i j -> p (h n) (i j)")
                pool.tensor_tensor(o, z[:, :, 0:PAIR // 2], z[:, :, PAIR // 2:], ALU.add).then_inc(z4_s, 1)

            def add_bias_term(g, c):
                pool.wait_ge(t_s, HALF * g + c + 1)
                after(pool, x1_s, HALF * g)
                pool.tensor_tensor(half(xt_sb, c), x_sb[:, (g * BG + BH * c) * L:(g * BG + BH * (c + 1)) * L],
                                   half(t_sb, c), ALU.add).then_inc(xt_s, 1)

            for slot in range(G * H + HALVE_LATER):
                g, h = divmod(slot, H)
                if g < G:
                    pairs(g, h)
                for q in range(QUADS):
                    for p in due(slot, (QH * q, 0), HALVE_LATER):
                        halve(p, q)
                for c in range(HALF):
                    for p in due(slot, AT_XT, c):
                        add_bias_term(p, c)

        @block.scalar
        def _(act):
            act.dma_start(g_raw[:, 0:1], g_xattn.partition_broadcast(P)).then_inc(g_in, 16)
            act.dma_start(g_raw[:, 1:2], g_ffn.partition_broadcast(P)).then_inc(g_in, 16)
            act.dma_start(bias_sb[:], bias.rearrange("(s o) -> s o", o=1)).then_inc(g_in, 16)
            act.dma_start(wr_f[:], wr.rearrange("(n p) e -> p n e", p=P)).then_inc(small_in, 16)
            act.dma_start(be_sb[:], be).then_inc(small_in, 16)
            act.wait_ge(g_in, 48)
            act.activation(g_tanh[:], g_raw[:], ACT.Tanh).then_inc(tanh_s, 1)

            def root(g):
                o = slice(BG * g, BG * (g + 1))
                act.wait_ge(eps_s, 1)
                act.wait_ge(mv_s, BG * (g + 1))
                act.activation(sd[:, o], mv[:, o, 1], ACT.Sqrt, bias=eps[:]).then_inc(sd_s, 1)

            def normalise(g):
                act.wait_ge(shift_s, g + 1)
                if g > 0:
                    act.wait_ge(turn_s, turn_count(V, g - 1, 1))
                    act.wait_ge(w_s, HALF * g)
                for b in range(BG):
                    n = g * BG + b
                    act.activation(v_sb[:, b], x_sb[:, n * L:(n + 1) * L], ACT.Identity,
                                   bias=shift[:, n:n + 1], scale=rstd[:, n:n + 1]).then_inc(v_s, 1)

            def keep(kind, dst, g, c):
                act.wait_ge(turn_s, turn_count(kind, g, c))
                after(act, kv_s, H * (g - 1))
                after(act, z_s, H * (g - 1))
                act.activation(dst[:, g % 2, :, BH * c:BH * (c + 1), :],
                               T[c][:].rearrange("p (n b) s -> p n b s", n=LB), ACT.Copy).then_inc(vcT_s, 1)

            def root1(g, c):
                o = slice(BH * c, BH * (c + 1))
                act.wait_ge(mv1_s, BG * g + BH * (c + 1))
                after(act, rstd1_s, HALF * g)
                act.activation(sd1[:, o], mv1[:, o, 1], ACT.Sqrt, bias=eps[:]).then_inc(sd1_s, 1)

            def round_xn(g, c):
                act.wait_ge(turn_s, turn_count(XN, g, c))
                after(act, m_s, UNITS * (g - 1))
                act.activation(xnT_hi[:, g % 2, BH * c:BH * (c + 1)].rearrange("p b n s -> p (b n) s"), T[c][:],
                               ACT.Copy).then_inc(xhi_s, 1)

            def logistic(g):
                act.wait_ge(diff_s, g + 1)
                act.activation(tdiff[:], diff[:], ACT.Tanh, scale=0.5).then_inc(tdiff_s, 1)

            def keep_gates(g):
                act.wait_ge(gT_s, g + 1)
                after(act, zb_s, HALF * g)
                act.activation(gateT[:], R[0:E, :].rearrange("e (b s) -> e b s", b=BG), ACT.Copy).then_inc(gTc_s, 1)

            root(0)
            normalise(0)
            for kind, dst in ((V, vT), (C, cT)):
                for c in range(HALF):
                    keep(kind, dst, 0, c)
            for slot in range(SLOTS):
                for g in due(slot, AT_ROOT1):
                    root1(g, 0)
                    root1(g, 1)
                for g in due(slot, AT_ROOT):
                    root(g)
                for g in due(slot, AT_NORM):
                    normalise(g)
                for g in due(slot, AT_ROUND):
                    round_xn(g, 0)
                    round_xn(g, 1)
                for g in due(slot, AT_TOP):
                    logistic(g)
                for g in due(slot, AT_V):
                    keep(V, vT, g, 0)
                    keep(V, vT, g, 1)
                for g in due(slot, AT_C):
                    keep(C, cT, g, 0)
                    keep(C, cT, g, 1)
                for g in due(slot, AT_GATES_T):
                    keep_gates(g)
                if slot == 0:
                    act.wait_ge(we_in, 16 * LB)
                    for n in range(WCH):
                        act.activation(piece(we_hi, n), piece(we_f, n), ACT.Copy).then_inc(we_hi_s, 1)
                    act.wait_ge(small_in, 32)
                    act.activation(wr_hi[:], wr_f[:], ACT.Copy).then_inc(wr_hi_s, 1)

        @block.tensor
        def _(pe):
            pe.wait_ge(ident_s, 1)

            def claim(kind, g, c):
                n = TURNS.index((kind, g)) - 1
                if n >= 0:
                    before, p = TURNS[n]
                    if before == V:
                        pe.wait_ge(vcT_s, 4 * p + c + 1)
                    elif before == C:
                        pe.wait_ge(vcT_s, 4 * p + HALF + c + 1)
                    elif before == SKIP:
                        pe.wait_ge(t_s, HALF * p + c + 1)
                    elif before == MIX:
                        pe.wait_ge(x1_s, HALF * p + c + 1)
                    else:
                        pe.wait_ge(xlo_s, HALF * p + c + 1)

            def turn4(c, blocks):
                for n, block_ in enumerate(blocks):
                    last = pe.transpose(T[c][:, n, :], block_, ident[:])
                last.then_inc(turn_s, 1)

            def transpose_v(g, c):
                pe.wait_ge(v_s, BG * g + BH * (c + 1))
                claim(V, g, c)
                turn4(c, [v_sb[:, b, P * n:P * (n + 1)] for n in range(LB) for b in range(BH * c, BH * (c + 1))])

            def transpose_c(g, c):
                pe.wait_ge(ctx_s, 16 * (g + 1))
                claim(C, g, c)
                turn4(c, [ctx_sb[:, b, P * n:P * (n + 1)] for n in range(LB) for b in range(BH * c, BH * (c + 1))])

            def sum_heads(g, c):
                if g == 0:
                    pe.wait_ge(ones_s, 1)
                pe.wait_ge(w_s, HALF * g + c + 1)
                claim(SKIP, g, c)
                pe.matmul(T[c][:].rearrange("p n s -> p (n s)"), head_ones[:], half(w_sb, c),
                          start=True, stop=True).then_inc(turn_s, 1)

            def conv(g, h):
                if g == 0 and h % QH == 0:
                    pe.wait_ge(toep_s[h // QH], 16)
                pe.wait_ge(kv_s, H * g + h + 1)
                after(pe, z_s, H * g + h - 2)
                y = Y[(H * g + h) % 3][:].rearrange("p n q -> p (n q)")
                m = kv[:, h % KVS].rearrange("p n i j -> p (n i j)")
                lower = BG * PAIR
                pe.matmul(y, toep[:, h, 0:P], m, start=True, stop=False)
                pe.matmul(y[:, lower:], toep[:, h, P:L], m[:, 0:lower], start=False, stop=True).then_inc(y_s, 1)

            def unit(g, u):
                b, e = u // (E // 2), 2 * (u % (E // 2))
                if g == 0 and u == 0:
                    pe.wait_ge(we_lo_s, WCH)
                after(pe, add_s, UNITS * g + u - 1)
                o = M[u % 2][:]
                for n in range(LB):
                    pe.matmul(o, xnT_hi[:, g % 2, b, n], we_hi[:, n, e:e + 2], start=(n == 0), stop=False)
                    pe.matmul(o, xnT_hi[:, g % 2, b, n], we_lo[:, n, e:e + 2], start=False, stop=False)
                    last = pe.matmul(o, xnT_lo[:, g % 2, b, n], we_hi[:, n, e:e + 2], start=False, stop=(n == LB - 1))
                last.then_inc(m_s, 1)

            def transpose_mix(g, c):
                pe.wait_ge(mixT_s, QUADS * (g + 1))
                claim(MIX, g, c)
                turn4(c, [mixT[:, n * BG + b].rearrange("p h j -> p (h j)")
                                     for b in range(BH * c, BH * (c + 1)) for n in range(LB)])

            def transpose_xn(g, c):
                pe.wait_ge(xn_s, BG * g + BH * (c + 1))
                claim(XN, g, c)
                turn4(c, [xn[:, b, P * n:P * (n + 1)] for b in range(BH * c, BH * (c + 1)) for n in range(LB)])

            def route(g):
                if g == 0:
                    pe.wait_ge(wr_lo_s, 1)
                pe.wait_ge(xlo_s, HALF * (g + 1))
                after(pe, start_s, HALF * g)
                for b in range(BG):
                    terms = [(x_, w_, n) for n in range(LB) for x_ in (xnT_hi, xnT_lo) for w_ in (wr_hi, wr_lo)]
                    for t, (x_, w_, n) in enumerate(terms):
                        last = pe.matmul(R[:, E * b:E * (b + 1)], x_[:, g % 2, b, n], w_[:, n], start=(t == 0), stop=(t == len(terms) - 1))
                last.then_inc(logit_s, 1)

            def transpose_gates(g):
                pe.wait_ge(gate_s, g + 1)
                for b in range(BG):
                    last = pe.matmul(R[0:E, S * b:S * (b + 1)], gate[:, g % 2, b], ident[:], start=True, stop=True)
                last.then_inc(gT_s, 1)

            def expert_bias(g, c):
                if g == 0:
                    pe.wait_ge(small_in, 32)
                pe.wait_ge(gTc_s, g + 1)
                after(pe, start_s, HALF * g + c)
                for b in range(BH):
                    last = pe.matmul(R[:, F * b:F * (b + 1)], gateT[:, BH * c + b], be_sb[:], start=True, stop=True)
                last.then_inc(zb_s, 1)

            for turn in (transpose_v, transpose_c, sum_heads):
                for c in range(HALF):
                    turn(0, c)
            for slot in range(SLOTS):
                g, h = divmod(slot, H)
                if g < G:
                    conv(g, h)
                for at, turn in ((AT_MIX, transpose_mix), (AT_XN, transpose_xn), (AT_V, transpose_v), (AT_C, transpose_c),
                                 (AT_SKIP, sum_heads)):
                    for p in due(slot, at):
                        turn(p, 0)
                        turn(p, 1)
                for p in due(slot, AT_ROUTE):
                    route(p)
                for p in due(slot, AT_GATES_T):
                    transpose_gates(p)
                for p in due(slot, AT_BIAS0):
                    expert_bias(p, 0)
                for p in due(slot, AT_BIAS1):
                    expert_bias(p, 1)
                for p, u in unit_at(slot):
                    unit(p, u)

        @block.vector
        def _(dve):
            dve.memset(eps[:], EPS).then_inc(eps_s, 1)

            def row_stats(b):
                dve.bn_stats(stats[:, b], x_sb[:, L * b:L * (b + 1)]).then_inc(stats_s, 1)
                dve.wait_ge(stats_s, b + 1)
                dve.bn_aggr(mv[:, b], stats[:, b]).then_inc(mv_s, 1)

            def scales(g):
                o = slice(BG * g, BG * (g + 1))
                dve.wait_ge(sd_s, g + 1)
                dve.reciprocal(rstd[:, o], sd[:, o]).then_inc(rstd_s, 1)
                dve.wait_ge(rstd_s, g + 1)
                dve.scalar_tensor_tensor(out=shift[:, o], in0=mv[:, o, 0], scalar=-1.0, in1=rstd[:, o],
                                         op0=ALU.mult, op1=ALU.mult).then_inc(shift_s, 1)

            def products(g, c):
                dve.wait_ge(ctx_s, 16 * (g + 1))
                dve.wait_ge(v_s, BG * g + BH * (c + 1))
                if g > 0:
                    dve.wait_ge(turn_s, turn_count(SKIP, g - 1, c))
                dve.scalar_tensor_tensor(out=half(w_sb, c), in0=half(v_sb, c), scalar=bias_g[:], in1=half(ctx_sb, c),
                                         op0=ALU.mult, op1=ALU.mult).then_inc(w_s, 1)

            def bias_term(g, c):
                dve.wait_ge(turn_s, turn_count(SKIP, g, c))
                after(dve, xt_s, HALF * (g - 1) + c + 1)
                dve.tensor_tensor(half(t_sb, c), T[c][:].rearrange("p n s -> p (n s)"),
                                  half(ctx_sb, c), ALU.mult).then_inc(t_s, 1)

            def weigh(g, h):
                dve.wait_ge(y_s, H * g + h + 1)
                q = h // QH
                if h % QH == 0:
                    after(dve, z4_s, QUADS * g + q - 1)
                ci = cT[:, g % 2, :, :, J * h:J * (h + 1)].rearrange("p n b i -> p (n b) i").unsqueeze(3)
                dve.tensor_tensor(z_sb[:, q % 2, h % QH], Y[(H * g + h) % 3][:].rearrange("p n (i j) -> p n i j", i=J),
                                  ci.broadcast_to([P, LB * BG, J, J]), ALU.mult).then_inc(z_s, 1)

            def reduce(g, q):
                dve.wait_ge(z4_s, QUADS * g + q + 1)
                after(dve, mixT_s, QUADS * g + q)
                z = z4[:, q % 2].rearrange("p h n i j -> p (h n) (i j)")
                dve.tensor_tensor(z2[:].rearrange("p h n i j -> p (h n) (i j)"), z[:, :, 0:2 * J], z[:, :, 2 * J:],
                                  ALU.add).then_inc(z2_s, 1)
                dve.wait_ge(z2_s, QUADS * g + q + 1)
                if q == 0 and g > 0:
                    dve.wait_ge(turn_s, turn_count(MIX, g - 1, 1))
                a, b = (z2[:, :, :, i].rearrange("p h n j -> p n h j") for i in range(2))
                dve.tensor_tensor(mixT[:, :, QH * q:QH * (q + 1)], a, b, ALU.add).then_inc(mixT_s, 1)

            def residual(g, c):
                dve.wait_ge(turn_s, turn_count(MIX, g, c))
                dve.wait_ge(xt_s, HALF * g + c + 1)
                after(dve, start_s, HALF * g)
                dve.scalar_tensor_tensor(out=half(x1, c), in0=T[c][:].rearrange("p n s -> p (n s)"),
                                         scalar=g_tanh[:, 0:1], in1=half(xt_sb, c), op0=ALU.mult, op1=ALU.add).then_inc(x1_s, 1)

            def row_stats1(g, c):
                dve.wait_ge(x1_s, HALF * g + c + 1)
                for b in range(BH * c, BH * (c + 1)):
                    dve.bn_stats(stats1[:, b], x1[:, b]).then_inc(stats1_s, 1)
                for b in range(BH * c, BH * (c + 1)):
                    dve.wait_ge(stats1_s, BG * g + b + 1)
                    dve.bn_aggr(mv1[:, b], stats1[:, b]).then_inc(mv1_s, 1)

            def normalise1(g, c):
                o = slice(BH * c, BH * (c + 1))
                dve.wait_ge(sd1_s, HALF * g + c + 1)
                dve.reciprocal(rstd1[:, o], sd1[:, o]).then_inc(rstd1_s, 1)
                dve.wait_ge(rstd1_s, HALF * g + c + 1)
                if g > 0:
                    dve.wait_ge(turn_s, turn_count(XN, g - 1, c))
                for b in range(BH * c, BH * (c + 1)):
                    dve.tensor_scalar(xn[:, b], x1[:, b], mv1[:, b, 0:1], rstd1[:, b:b + 1],
                                      ALU.subtract, ALU.mult).then_inc(xn_s, 1)

            def rest_xn(g, c):
                dve.wait_ge(xhi_s, HALF * g + c + 1)
                o = slice(BH * c, BH * (c + 1))
                dve.tensor_tensor(xnT_lo[:, g % 2, o].rearrange("p b n s -> p (b n) s"), T[c][:],
                                  xnT_hi[:, g % 2, o].rearrange("p b n s -> p (b n) s"), ALU.subtract).then_inc(xlo_s, 1)

            def top_two(g):
                dve.wait_ge(logit_s, g + 1)
                dve.tensor_copy(logits[:], R[:, 0:BG * E].rearrange("p (b e) -> p b e", b=BG)).then_inc(lcopy_s, 1)
                dve.wait_ge(lcopy_s, g + 1)
                for b in range(BG):
                    dve.max(top8[:, b], logits[:, b]).then_inc(top_s, 1)
                for b in range(BG):
                    dve.wait_ge(top_s, BG * g + b + 1)
                    dve.max_index(idx8[:, b], top8[:, b], logits[:, b]).then_inc(idx_s, 1)
                dve.tensor_tensor(diff[:], top8[:, :, 0], top8[:, :, 1], ALU.subtract).then_inc(diff_s, 1)
                dve.wait_ge(idx_s, BG * (g + 1))
                dve.tensor_copy(idxf[:], idx8[:, :, 0:TOP]).then_inc(idxf_s, 1)

            def gates(g):
                dve.wait_ge(tdiff_s, g + 1)
                for k in range(TOP):
                    dve.tensor_scalar(wts[:, :, k], tdiff[:], g_half[:, k:k + 1], g_half[:, 0:1], ALU.mult, ALU.add).then_inc(wts_s, 1)
                dve.wait_ge(idxf_s, g + 1)
                dve.wait_ge(wts_s, TOP * (g + 1))
                for b in range(BG):
                    for k in range(TOP):
                        dve.tensor_scalar(gk[:, k, b], iota_e[:], idxf[:, b, k:k + 1], wts[:, b, k:k + 1],
                                          ALU.is_equal, ALU.mult).then_inc(gk_s, 1)
                dve.wait_ge(gk_s, BG * TOP * (g + 1))
                after(dve, add_s, UNITS * (g - 1))
                dve.tensor_tensor(gate[:, g % 2], gk[:, 0], gk[:, 1], ALU.add).then_inc(gate_s, 1)

            def start(g, c):
                dve.wait_ge(zb_s, HALF * g + c + 1)
                for b in range(BH * c, BH * (c + 1)):
                    after(dve, out_s[g % 2][b], 16 * (g // 2))
                dve.tensor_tensor(half(acc[:, g % 2], c), R[:], half(x1, c), ALU.add).then_inc(start_s, 1)

            def add(g, u):
                b, e = u // (E // 2), 2 * (u % (E // 2))
                dve.wait_ge(m_s, UNITS * g + u + 1)
                dve.wait_ge(start_s, HALF * g + u // (UNITS // HALF) + 1)
                after(dve, add_s, UNITS * g + u)
                dve.scalar_tensor_tensor(out=acc[:, g % 2, b], in0=M[u % 2][:, 0], scalar=gate[:, g % 2, b, e:e + 1], in1=acc[:, g % 2, b],
                                         op0=ALU.mult, op1=ALU.add).then_inc(acc_s, 1)
                dve.wait_ge(acc_s, UNITS * g + u + 1)
                dve.scalar_tensor_tensor(out=acc[:, g % 2, b], in0=M[u % 2][:, 1], scalar=gate[:, g % 2, b, e + 1:e + 2], in1=acc[:, g % 2, b],
                                         op0=ALU.mult, op1=ALU.add).then_inc(add_s, 1)

            dve.wait_ge(x_in[0], 16)
            for b in range(BG):
                row_stats(b)
            dve.wait_ge(tanh_s, 1)
            dve.tensor_tensor(bias_g[:], bias_sb[:], g_tanh[:, 0:1], ALU.mult).then_inc(gains_s, 1)
            for k, sign in enumerate((0.5, -0.5)):
                dve.tensor_scalar(g_half[:, k:k + 1], g_tanh[:, 1:2], sign, None, ALU.mult).then_inc(gains_s, 1)
            scales(0)
            dve.wait_ge(gains_s, 3)
            for step in (products, bias_term):
                for c in range(HALF):
                    step(0, c)
            for slot in range(SLOTS):
                g, h = divmod(slot, H)
                if g < G:
                    weigh(g, h)
                for b in range(BG):
                    for p in due(slot, AT_STATS, b):
                        if b == 0:
                            dve.wait_ge(x_in[p], 16)
                        row_stats(BG * p + b)
                for q in range(QUADS):
                    for p in due(slot, (QH * q, 0), REDUCE_LATER):
                        reduce(p, q)
                for c in range(HALF):
                    for p in due(slot, AT_RESIDUAL):
                        residual(p, c)
                    for p in due(slot, AT_RESIDUAL, c):
                        row_stats1(p, c)
                    for p in due(slot, AT_NORM1):
                        normalise1(p, c)
                for p in due(slot, AT_SCALES):
                    scales(p)
                for c in range(HALF):
                    for p in due(slot, AT_REST):
                        rest_xn(p, c)
                    for p in due(slot, AT_PRODUCTS, c):
                        products(p, c)
                    for p in due(slot, AT_TERM, c):
                        bias_term(p, c)
                for p in due(slot, AT_TOP):
                    top_two(p)
                for p in due(slot, AT_GATES):
                    gates(p)
                for p in due(slot, AT_START0):
                    start(p, 0)
                for p in due(slot, AT_START1):
                    start(p, 1)
                for p, u in unit_at(slot):
                    add(p, u)
                if 4 <= slot < 4 + 2 * WCH and slot % 2 == 0:
                    n = (slot - 4) // 2
                    dve.wait_ge(we_hi_s, n + 1)
                    dve.tensor_tensor(piece(we_lo, n), piece(we_f, n), piece(we_hi, n), ALU.subtract).then_inc(we_lo_s, 1)
                if slot == 4 + 2 * WCH:
                    dve.wait_ge(wr_hi_s, 1)
                    dve.tensor_tensor(wr_lo[:], wr_f[:], wr_hi[:], ALU.subtract).then_inc(wr_lo_s, 1)
                    dve.wait_ge(iota_s, 1)


def kernel(x, fside_S2_0, ctx_2048, g_xattn, g_ffn, L0_xattn_k, L0_ffn_Wr, L0_ffn_We, L0_ffn_be):
    import numpy as np
    import concourse.bacc as bacc
    from concourse.bass_utils import run_bass_kernel_spmd

    kpad = np.zeros((H, KPAD), np.float32)
    kpad[:, P:] = np.asarray(L0_xattn_k)
    toep = np.lib.stride_tricks.sliding_window_view(kpad, L, axis=1)[:, P:0:-1].transpose(1, 0, 2)
    arrays = {"x": x, "bias": fside_S2_0, "ctx": ctx_2048, "g_xattn": g_xattn, "g_ffn": g_ffn, "toep": toep,
              "wr": L0_ffn_Wr, "we": L0_ffn_We, "be": L0_ffn_be}
    arrays = {f"in_{n}": np.ascontiguousarray(a) for n, a in arrays.items()}
    nc = bacc.Bacc("TRN2", target_bir_lowering=False, num_devices=1)
    args = [nc.dram_tensor(n, a.shape, mybir.dt.from_np(a.dtype), kind="ExternalInput").ap() for n, a in arrays.items()]
    out = nc.dram_tensor("out_0", (B, S, F), F32, kind="ExternalOutput").ap()
    build(nc, *args, out)
    r = run_bass_kernel_spmd(nc, [arrays], core_ids=[0])
    return r.results[0]["out_0"]
```

```python
import concourse.bass as bass
from concourse import mybir
from concourse.alu_op_type import AluOpType as ALU
from contextlib import ExitStack

F32 = mybir.dt.float32
F32R = mybir.dt.float32r
U32 = mybir.dt.uint32
ACT = mybir.ActivationFunctionType

P = 128
B, S, L = 16, 128, 256
H = 16
J = S // H
E, F = 8, 256
PARTS = 3
TOP = 2
EPS = 1e-5
BG = 4
G = B // BG
LB = L // P
PAIR = J * J
HALF = 2
BH = BG // HALF
QUADS = 4
QH = H // QUADS
UNITS = BG * E // 2
KPAD = P + L

LAG = 15
SLOTS = H + LAG + G * UNITS
KVS = 8
Y_BANKS, UNIT_BANKS = 3, 2
TAIL = G * H - (H + LAG) + 1
WARM_UP = 18
WCH = 8
WCW = LB * E * F // WCH

AT_STATS, AT_ROOT, AT_SCALES, AT_NORM = (0, 1), (2, 1), (5, 1), (5, 1)
AT_PRODUCTS, AT_V, AT_C = (10, 1), (10, 1), (14, 1)
AT_WROUND, AT_WREST, AT_SKIP, AT_TERM, AT_XT = (11, 1), (12, 1), (15, 1), (14, 1), (15, 0)
AT_MIX, AT_RESIDUAL, AT_ROOT1, AT_NORM1 = (4, -1), (4, -1), (5, -1), (6, -1)
AT_XN, AT_ROUND, AT_REST = (9, -1), (9, -1), (8, -1)
AT_ROUTE, AT_TOP, AT_GATES, AT_GATES_T = (10, -1), (10, -1), (11, -1), (14, -1)
AT_BIAS0, AT_START0, AT_BIAS1, AT_START1 = (15, -1), (15, -1), (1, -2), (1, -2)
FIRST_WROUND, FIRST_WREST, FIRST_SKIP, FIRST_TERM = 0, 0, 6, 6
WE_ROUND, WE_REST = 4, 6
HALVE_LATER, REDUCE_LATER = 7, 6


def due(slot, at, later=0):
    g, h = divmod(slot - later, H)
    return (g + at[1],) if slot >= later and h == at[0] and 0 <= g + at[1] < G else ()


def bias_due(slot, at, first, later=0):
    return due(slot, at, later) + ((0,) if slot - later == first else ())


def unit_at(slot):
    k = slot - H - LAG
    return (divmod(k, UNITS),) if 0 <= k < G * UNITS else ()


def unit_bank(k):
    return k % UNIT_BANKS if k < TAIL else (k - TAIL) % (UNIT_BANKS + Y_BANKS)


def bank_before(k):
    return max((j + 1 for j in range(k) if unit_bank(j) == unit_bank(k)), default=0)


V, C, SKIP, MIX, XN = "v", "ctx", "skip", "mix", "xn"
TURNS = [(C, 0), (V, 0)]
for _slot in range(SLOTS):
    for _kind, _at in ((MIX, AT_MIX), (XN, AT_XN), (V, AT_V), (C, AT_C)):
        TURNS += [(_kind, _g) for _g in due(_slot, _at)]
    TURNS += [(SKIP, _g) for _g in bias_due(_slot, AT_SKIP, FIRST_SKIP)]


def turn_count(kind, g, c):
    return HALF * TURNS.index((kind, g)) + c + 1


def build(nc, x, bias, ctx_in, g_xattn, g_ffn, toep_in, wr, we, be, out):
    es = ExitStack()
    with es:
        def sb(name, shape, dt=F32):
            return es.enter_context(nc.sbuf_tensor(name, shape, dt))

        def sem(name):
            return es.enter_context(nc.semaphore(name))

        def bank(name, shape):
            return es.enter_context(nc.psum_tensor(name, shape, F32))

        ident = sb("ident", [P, P])
        head_ones = sb("head_ones", [P, P])
        head_ones_r = sb("head_ones_r", [P, P], F32R)
        toep = sb("toep", [P, H, L])
        we_f = sb("we_f", [P, LB, E, F])
        we_hi = sb("we_hi", [P, LB, E, F], F32R)
        we_lo = sb("we_lo", [P, LB, E, F], F32R)
        wr_f = sb("wr_f", [P, LB, E])
        wr_parts = sb("wr_parts", [P, LB, 2, E], F32R)
        be_f = sb("be_f", [PARTS * BG * E, BG, F])
        be_r = sb("be_r", [PARTS * BG * E, BG, F], F32R)
        bias_sb = sb("bias_sb", [P, 1])
        bias_g = sb("bias_g", [P, 1])
        g_raw = sb("g_raw", [P, 2])
        g_tanh = sb("g_tanh", [P, 2])
        g_half = sb("g_half", [P, 2])
        eps = sb("eps", [P, 1])
        table_probe = sb("table_probe", [P, 1])
        iota_e = sb("iota_e", [P, E])

        x_sb = sb("x_sb", [P, B * L])
        stats = sb("stats", [P, B, 6])
        mv = sb("mv", [P, B, 2])
        sd = sb("sd", [P, B])
        rstd = sb("rstd", [P, B])
        shift = sb("shift", [P, B])
        ctx_sb = sb("ctx_sb", [P, BG, L])
        v_sb = sb("v_sb", [P, BG, L])
        w_sb = sb("w_sb", [P, BG, L])
        w_hi = sb("w_hi", [P, BG, L], F32R)
        w_lo = sb("w_lo", [P, BG, L], F32R)
        t_sb = sb("t_sb", [P, BG, L])
        xt_sb = sb("xt_sb", [P, BG, L])
        vT = sb("vT", [P, 2, LB, BG, S])
        cT = sb("cT", [P, 2, LB, BG, S])
        kv = sb("kv", [P, KVS, LB * BG, J, J])
        z_sb = sb("z_sb", [P, 2, QH, LB * BG, J, J])
        z4 = sb("z4", [P, 2, QH, LB * BG, J // 2, J])
        z2 = sb("z2", [P, QH, LB * BG, J // 4, J])
        mixT = sb("mixT", [P, LB * BG, H, J])

        x1 = sb("x1", [P, BG, L])
        stats1 = sb("stats1", [P, BG, 6])
        mv1 = sb("mv1", [P, BG, 2])
        sd1 = sb("sd1", [P, BG])
        rstd1 = sb("rstd1", [P, BG])
        shift1 = sb("shift1", [P, BG])
        xn = sb("xn", [P, BG, L])
        xnT_hi = sb("xnT_hi", [P, 2, BG, LB, S], F32R)
        xnT_lo = sb("xnT_lo", [P, 2, BG, LB, S], F32R)
        logits_hi = sb("logits_hi", [P, BG, E])
        logits = sb("logits", [P, BG, E])
        top8 = sb("top8", [P, BG, 8])
        idx8 = sb("idx8", [P, BG, 8], U32)
        idxf = sb("idxf", [P, BG, TOP])
        diff = sb("diff", [P, BG])
        tdiff = sb("tdiff", [P, BG])
        wts = sb("wts", [P, BG, TOP])
        hit = sb("hit", [P, BG * TOP, E])
        gk = sb("gk", [P, BG, TOP, E])
        gate = sb("gate", [P, 2, BG, E])
        gate_parts = sb("gate_parts", [P, PARTS, BG, E])
        gate_r = sb("gate_r", [P, BG, E], F32R)
        gateT = sb("gateT", [PARTS * BG * E, S], F32R)
        acc = we_f[:, 0].rearrange("p (n b) f -> p n b f", n=2)

        Y = [bank(f"Y{n}", [P, LB * BG, PAIR]) for n in range(Y_BANKS)]
        M = [bank(f"M{n}", [P, 2, F]) for n in range(UNIT_BANKS)]
        T = [bank(f"T{n}", [P, 4, P]) for n in range(HALF)]
        R = bank("R", [P, BH * F])

        x_half_in = [sem(f"x_half_loaded{c}") for c in range(HALF)]
        x_in, ctx_s = [sem(f"x_loaded{g}") for g in range(G)], sem("ctx_loaded")
        toep_s = [sem(f"toep_loaded{q}") for q in range(QUADS)]
        we_in, wr_in, g_in = [sem(f"we_loaded{n}") for n in range(LB)], sem("wr_loaded"), sem("gains_loaded")
        ident0, ident_s = sem("ident_zeroed"), sem("ident_ready")
        ones0, ones1, ones_s = sem("ones_filled"), sem("ones_cut"), sem("ones_ready")
        ones_r_s = sem("head_ones_ready")
        iota_s, eps_s, tanh_s, gains_s = sem("iota_ready"), sem("eps_ready"), sem("tanh_ready"), sem("gains_ready")
        we_hi_s, we_lo_s = sem("we_hi_ready"), sem("we_lo_ready")
        wr_hi_s, wr_lo_s = sem("wr_hi_ready"), sem("wr_lo_ready")
        stats_s, mv_s, sd_s = sem("stats_ready"), sem("mean_var_ready"), sem("sd_ready")
        rstd_s, shift_s = sem("rstd_ready"), sem("shift_ready")
        v_s, w_s, w_hi_s, w_lo_s = sem("v_ready"), sem("w_ready"), sem("w_hi_ready"), sem("w_lo_ready")
        t_s, xt_s = sem("bias_term_ready"), sem("xt_ready")
        turn_s = sem("turn_ready")
        vT_s, cT_s = sem("vT_ready"), sem("cT_ready")
        first_kv_s, kv_s, y_s, z_s = sem("first_kv_ready"), sem("kv_ready"), sem("y_ready"), sem("z_ready")
        z4_s, z2_s, mixT_s = sem("z4_ready"), sem("z2_ready"), sem("mixT_ready")
        x1_s, stats1_s, mv1_s = sem("x1_ready"), sem("stats1_ready"), sem("mean_var1_ready")
        sd1_s, rstd1_s, shift1_s, xn_s = sem("sd1_ready"), sem("rstd1_ready"), sem("shift1_ready"), sem("xn_ready")
        xhi_s, xlo_s = sem("xnT_hi_ready"), sem("xnT_lo_ready")
        logit_s, lhi_s, lcopy_s, top_s, idx_s = sem("logit_parts_ready"), sem("logits_hi_ready"), sem("logits_ready"), sem("top_ready"), sem("index_ready")
        idxf_s, diff_s, tdiff_s, wts_s = sem("idxf_ready"), sem("diff_ready"), sem("tdiff_ready"), sem("weights_ready")
        hit_s, gk_s, gate_s = sem("hit_ready"), sem("gate_of_k_ready"), sem("gate_ready")
        gate_r_s, gate_p_s = sem("gate_rounded"), sem("gate_parts_ready")
        be_zero, be_in, be_hi_s, be_s = sem("be_zeroed"), sem("be_loaded"), sem("be_rounded"), sem("be_ready")
        gT_s, gTc_s, zb_s = sem("gateT_in_psum"), sem("gateT_ready"), sem("expert_bias_ready")
        start_s, acc_s, add_s = sem("acc_started"), sem("acc_half_added"), sem("unit_added")
        m_s = sem("unit_ready")
        out_s = [[sem(f"out_stored{n}_{b}") for b in range(BG)] for n in range(2)]

        def after(eng, s, n):
            if n > 0:
                eng.wait_ge(s, n)

        def half(t, c):
            return t[:, BH * c:BH * (c + 1)].rearrange("p b l -> p (b l)")

        def pairs(eng, g, h):
            if h < 2:
                eng.wait_ge(vT_s, HALF * (g + 1))
                eng.wait_ge(cT_s, HALF * (g + 1))
            after(eng, y_s, H * g + h - KVS + 1)
            s = slice(J * h, J * (h + 1))
            vi = vT[:, g % 2, :, :, s].rearrange("p n b i -> p (n b) i").unsqueeze(3).broadcast_to([P, LB * BG, J, J])
            cj = cT[:, g % 2, :, :, s].rearrange("p n b i -> p (n b) i").unsqueeze(2).broadcast_to([P, LB * BG, J, J])
            return eng.tensor_tensor(kv[:, h % KVS], vi, cj, ALU.mult)

        def unit_psum(k):
            n = unit_bank(k)
            return M[n][:] if n < UNIT_BANKS else Y[n - UNIT_BANKS][:].rearrange("p (k n) q -> p k (n q)", k=2)

        def piece(t, n):
            return t[:].rearrange("p n e f -> p (n e f)")[:, WCW * n:WCW * (n + 1)]

        block = es.enter_context(nc.Block())

        @block.sync
        def _(sp):
            def load_x(g):
                sp.dma_start(x_sb[:, g * BG * L:(g + 1) * BG * L].rearrange("p (b l) -> p b l", l=L),
                             x[g * BG:(g + 1) * BG].rearrange("b s l -> s b l")).then_inc(x_in[g], 16)

            def load_ctx(g):
                after(sp, t_s, HALF * g)
                sp.dma_start(ctx_sb[:], ctx_in[g * BG:(g + 1) * BG].rearrange("b s l -> s b l")).then_inc(ctx_s, 16)

            def load_toep(q):
                sp.dma_start(toep[:, QH * q:QH * (q + 1), :], toep_in[:, QH * q:QH * (q + 1), :]).then_inc(toep_s[q], 16)

            for c in range(HALF):
                sp.dma_start(x_sb[:, c * BH * L:(c + 1) * BH * L].rearrange("p (b l) -> p b l", l=L),
                             x[c * BH:(c + 1) * BH].rearrange("b s l -> s b l")).then_inc(x_half_in[c], 16)
            load_ctx(0)
            load_toep(0)
            sp.dma_start(g_raw[:, 0:1], g_xattn.partition_broadcast(P)).then_inc(g_in, 16)
            sp.dma_start(g_raw[:, 1:2], g_ffn.partition_broadcast(P)).then_inc(g_in, 16)
            sp.dma_start(bias_sb[:], bias.rearrange("(s o) -> s o", o=1)).then_inc(g_in, 16)
            sp.dma_start(wr_f[:], wr.rearrange("(n p) e -> p n e", p=P)).then_inc(wr_in, 16)
            load_toep(1)
            load_x(1)
            load_toep(2)
            load_toep(3)
            for n in range(LB):
                sp.dma_start(we_f[:, n], we[:, P * n:P * (n + 1)].rearrange("e p f -> p e f")).then_inc(we_in[n], 16)
            for g in range(2, G):
                load_x(g)
            sp.wait_ge(be_zero, 1)
            for n in range(PARTS * BG):
                sp.dma_start(be_f[E * n:E * (n + 1), n % BG], be).then_inc(be_in, 16)
            for slot in range(SLOTS):
                for g in bias_due(slot, AT_TERM, FIRST_TERM, 2):
                    if g + 1 < G:
                        load_ctx(g + 1)
                for g, u in unit_at(slot):
                    if u % (UNITS // BG) == UNITS // BG - 1:
                        b = u // (UNITS // BG)
                        sp.wait_ge(add_s, UNITS * g + u + 1)
                        sp.dma_start(out[g * BG + b], acc[:, g % 2, b, :]).then_inc(out_s[g % 2][b], 16)
            for g in (G - 2, G - 1):
                for b in range(BG):
                    sp.wait_ge(out_s[g % 2][b], 16 * (g // 2 + 1))

        @block.gpsimd
        def _(pool):
            pool.memset(ident[:], 0.0).then_inc(ident0, 1)
            pool.memset(be_f[:], 0.0).then_inc(be_zero, 1)
            pool.wait_ge(ident0, 1)
            pool.affine_select(out=ident[:], in_=ident[:], compare_op=ALU.not_equal, fill=1.0, base=0,
                               pattern=[[-1, P]], channel_multiplier=1).then_inc(ident_s, 1)
            pool.memset(head_ones[:], 1.0).then_inc(ones0, 1)
            pool.wait_ge(ones0, 1)
            pool.affine_select(out=head_ones[:], in_=head_ones[:], compare_op=ALU.is_ge, fill=0.0, base=0,
                               pattern=[[-J, H], [0, J]], channel_multiplier=1).then_inc(ones1, 1)
            pool.wait_ge(ones1, 1)
            pool.affine_select(out=head_ones[:], in_=head_ones[:], compare_op=ALU.is_ge, fill=0.0, base=J - 1,
                               pattern=[[J, H], [0, J]], channel_multiplier=-1).then_inc(ones_s, 1)
            pool.iota(iota_e[:], [[1, E]], base=0, channel_multiplier=0,
                      allow_small_or_imprecise_dtypes=True).then_inc(iota_s, 1)

            def halve(g, q):
                pool.wait_ge(z_s, H * g + QH * (q + 1))
                after(pool, z2_s, QUADS * g + q - 1)
                z = z_sb[:, q % 2].rearrange("p h n i j -> p (h n) (i j)")
                o = z4[:, q % 2].rearrange("p h n i j -> p (h n) (i j)")
                pool.tensor_tensor(o, z[:, :, 0:PAIR // 2], z[:, :, PAIR // 2:], ALU.add).then_inc(z4_s, 1)

            def add_bias_term(g, c):
                pool.wait_ge(t_s, HALF * g + c + 1)
                after(pool, x1_s, HALF * g)
                pool.tensor_tensor(half(xt_sb, c), x_sb[:, (g * BG + BH * c) * L:(g * BG + BH * (c + 1)) * L],
                                   half(t_sb, c), ALU.add).then_inc(xt_s, 1)

            for slot in range(G * H + HALVE_LATER):
                g, h = divmod(slot, H)
                if 0 < slot < G * H:
                    pairs(pool, g, h).then_inc(kv_s, 1)
                for q in range(QUADS):
                    for p in due(slot, (QH * q, 0), HALVE_LATER):
                        halve(p, q)
                for c in range(HALF):
                    for p in due(slot, AT_XT, c):
                        add_bias_term(p, c)

        @block.scalar
        def _(act):
            def root(g, c):
                o = slice(BG * g + BH * c, BG * g + BH * (c + 1))
                act.wait_ge(eps_s, 1)
                act.wait_ge(mv_s, BG * g + BH * (c + 1))
                act.activation(sd[:, o], mv[:, o, 1], ACT.Sqrt, bias=eps[:]).then_inc(sd_s, 1)

            def normalise(g, c):
                act.wait_ge(shift_s, HALF * g + c + 1)
                if g > 0:
                    act.wait_ge(turn_s, turn_count(V, g - 1, 1))
                    act.wait_ge(w_s, HALF * g)
                for b in range(BH * c, BH * (c + 1)):
                    n = g * BG + b
                    act.activation(v_sb[:, b], x_sb[:, n * L:(n + 1) * L], ACT.Identity,
                                   bias=shift[:, n:n + 1], scale=rstd[:, n:n + 1]).then_inc(v_s, 1)

            def keep(kind, dst, g, c):
                act.wait_ge(turn_s, turn_count(kind, g, c))
                after(act, kv_s, H * (g - 1) - 1)
                after(act, z_s, H * (g - 1))
                act.activation(dst[:, g % 2, :, BH * c:BH * (c + 1), :],
                               T[c][:].rearrange("p (n b) s -> p n b s", n=LB), ACT.Copy).then_inc(vT_s if kind == V else cT_s, 1)

            def round_w(g, c):
                act.wait_ge(w_s, HALF * g + c + 1)
                if g > 0:
                    act.wait_ge(turn_s, turn_count(SKIP, g - 1, c))
                act.activation(half(w_hi, c), half(w_sb, c), ACT.Copy).then_inc(w_hi_s, 1)

            def root1(g, c):
                o = slice(BH * c, BH * (c + 1))
                act.wait_ge(mv1_s, BG * g + BH * (c + 1))
                after(act, rstd1_s, HALF * g)
                act.activation(sd1[:, o], mv1[:, o, 1], ACT.Sqrt, bias=eps[:]).then_inc(sd1_s, 1)

            def normalise1(g, c):
                act.wait_ge(shift1_s, HALF * g + c + 1)
                if g > 0:
                    act.wait_ge(turn_s, turn_count(XN, g - 1, c))
                for b in range(BH * c, BH * (c + 1)):
                    act.activation(xn[:, b], x1[:, b], ACT.Identity, bias=shift1[:, b:b + 1], scale=rstd1[:, b:b + 1]).then_inc(xn_s, 1)

            def round_xn(g, c):
                act.wait_ge(turn_s, turn_count(XN, g, c))
                after(act, m_s, UNITS * (g - 1))
                act.activation(xnT_hi[:, g % 2, BH * c:BH * (c + 1)].rearrange("p b n s -> p (b n) s"), T[c][:],
                               ACT.Copy).then_inc(xhi_s, 1)

            def logistic(g):
                act.wait_ge(diff_s, g + 1)
                act.activation(tdiff[:], diff[:], ACT.Tanh, scale=0.5).then_inc(tdiff_s, 1)

            def keep_gates(g):
                act.wait_ge(gT_s, g + 1)
                after(act, zb_s, HALF * g)
                act.activation(gateT[:], R[0:PARTS * BG * E, 0:S], ACT.Copy).then_inc(gTc_s, 1)

            act.wait_ge(eps_s, 1)
            act.activation(table_probe[:], eps[:], ACT.Sqrt)
            root(0, 0)
            root(0, 1)
            normalise(0, 0)
            normalise(0, 1)
            for c in range(HALF):
                keep(V, vT, 0, c)
            act.wait_ge(g_in, 48)
            act.activation(g_tanh[:], g_raw[:], ACT.Tanh).then_inc(tanh_s, 1)
            for slot in range(SLOTS):
                for g in due(slot, AT_ROOT1):
                    root1(g, 0)
                    root1(g, 1)
                for g in due(slot, AT_ROOT):
                    root(g, 0)
                    root(g, 1)
                for g in due(slot, AT_NORM):
                    normalise(g, 0)
                    normalise(g, 1)
                for g in due(slot, AT_NORM1):
                    normalise1(g, 0)
                    normalise1(g, 1)
                for g in due(slot, AT_ROUND):
                    round_xn(g, 0)
                    round_xn(g, 1)
                for g in due(slot, AT_TOP):
                    logistic(g)
                for g in bias_due(slot, AT_WROUND, FIRST_WROUND):
                    round_w(g, 0)
                    round_w(g, 1)
                for g in due(slot, AT_V):
                    keep(V, vT, g, 0)
                    keep(V, vT, g, 1)
                for g in due(slot, AT_C):
                    keep(C, cT, g, 0)
                    keep(C, cT, g, 1)
                for g in due(slot, AT_GATES_T):
                    keep_gates(g)
                if 0 <= slot - WE_ROUND < WCH:
                    n = slot - WE_ROUND
                    act.wait_ge(we_in[n // (WCH // LB)], 16)
                    act.activation(piece(we_hi, n), piece(we_f, n), ACT.Copy).then_inc(we_hi_s, 1)
                if slot == WE_ROUND + WCH:
                    act.wait_ge(wr_in, 16)
                    act.activation(wr_parts[:, :, 0], wr_f[:], ACT.Copy).then_inc(wr_hi_s, 1)
                    act.wait_ge(be_in, 16 * PARTS * BG)
                    act.activation(be_r[:].rearrange("p b f -> p (b f)"), be_f[:].rearrange("p b f -> p (b f)"), ACT.Copy).then_inc(be_hi_s, 1)

        @block.tensor
        def _(pe):
            pe.wait_ge(ident_s, 1)

            def claim(kind, g, c):
                n = TURNS.index((kind, g)) - 1
                if n >= 0:
                    before, p = TURNS[n]
                    if before == V:
                        pe.wait_ge(vT_s, HALF * p + c + 1)
                    elif before == C:
                        pe.wait_ge(cT_s, HALF * p + c + 1)
                    elif before == SKIP:
                        pe.wait_ge(t_s, HALF * p + c + 1)
                    elif before == MIX:
                        pe.wait_ge(x1_s, HALF * p + c + 1)
                    else:
                        pe.wait_ge(xlo_s, HALF * p + c + 1)

            def turn4(c, blocks):
                for n, block_ in enumerate(blocks):
                    last = pe.transpose(T[c][:, n, :], block_, ident[:])
                last.then_inc(turn_s, 1)

            def transpose_v(g, c):
                pe.wait_ge(v_s, BG * g + BH * (c + 1))
                claim(V, g, c)
                turn4(c, [v_sb[:, b, P * n:P * (n + 1)] for n in range(LB) for b in range(BH * c, BH * (c + 1))])

            def transpose_c(g, c):
                pe.wait_ge(ctx_s, 16 * (g + 1))
                claim(C, g, c)
                turn4(c, [ctx_sb[:, b, P * n:P * (n + 1)] for n in range(LB) for b in range(BH * c, BH * (c + 1))])

            def sum_heads(g, c):
                if g == 0:
                    pe.wait_ge(ones_r_s, 1)
                pe.wait_ge(w_lo_s, HALF * g + c + 1)
                claim(SKIP, g, c)
                o = T[c][:].rearrange("p n s -> p (n s)")
                pe.matmul(o, head_ones_r[:], half(w_hi, c), start=True, stop=False)
                pe.matmul(o, head_ones_r[:], half(w_lo, c), start=False, stop=True).then_inc(turn_s, 1)

            def conv(g, h):
                if g == 0 and h % QH == 0:
                    pe.wait_ge(toep_s[h // QH], 16)
                if g == 0 and h == 0:
                    pe.wait_ge(first_kv_s, 1)
                after(pe, kv_s, H * g + h)
                after(pe, z_s, H * g + h + 1 - Y_BANKS)
                y = Y[(H * g + h) % Y_BANKS][:].rearrange("p n q -> p (n q)")
                m = kv[:, h % KVS].rearrange("p n i j -> p (n i j)")
                lower = BG * PAIR
                pe.matmul(y, toep[:, h, 0:P], m, start=True, stop=False)
                pe.matmul(y[:, lower:], toep[:, h, P:L], m[:, 0:lower], start=False, stop=True).then_inc(y_s, 1)

            def unit(g, u):
                b, e = u // (E // 2), 2 * (u % (E // 2))
                if g == 0 and u == 0:
                    pe.wait_ge(we_lo_s, WCH)
                k = UNITS * g + u
                after(pe, add_s, bank_before(k))
                if k >= TAIL and bank_before(k) == 0:
                    pe.wait_ge(z_s, G * H)
                o = unit_psum(k)
                for n in range(LB):
                    pe.matmul(o, xnT_hi[:, g % 2, b, n], we_hi[:, n, e:e + 2], start=(n == 0), stop=False)
                    pe.matmul(o, xnT_hi[:, g % 2, b, n], we_lo[:, n, e:e + 2], start=False, stop=False)
                    last = pe.matmul(o, xnT_lo[:, g % 2, b, n], we_hi[:, n, e:e + 2], start=False, stop=(n == LB - 1))
                last.then_inc(m_s, 1)

            def transpose_mix(g, c):
                pe.wait_ge(mixT_s, QUADS * (g + 1))
                claim(MIX, g, c)
                turn4(c, [mixT[:, n * BG + b].rearrange("p h j -> p (h j)")
                                     for b in range(BH * c, BH * (c + 1)) for n in range(LB)])

            def transpose_xn(g, c):
                pe.wait_ge(xn_s, BG * g + BH * (c + 1))
                claim(XN, g, c)
                turn4(c, [xn[:, b, P * n:P * (n + 1)] for b in range(BH * c, BH * (c + 1)) for n in range(LB)])

            def route(g):
                if g == 0:
                    pe.wait_ge(wr_lo_s, 1)
                pe.wait_ge(xlo_s, HALF * (g + 1))
                after(pe, start_s, HALF * g)
                for b in range(BG):
                    terms = [(x_, n) for n in range(LB) for x_ in (xnT_hi, xnT_lo)]
                    for t, (x_, n) in enumerate(terms):
                        last = pe.matmul(R[:, 2 * E * b:2 * E * (b + 1)], x_[:, g % 2, b, n], wr_parts[:, n].rearrange("p k e -> p (k e)"),
                                         start=(t == 0), stop=(t == len(terms) - 1))
                last.then_inc(logit_s, 1)

            def transpose_gates(g):
                pe.wait_ge(gate_p_s, 2 * (g + 1))
                pe.transpose(R[0:PARTS * BG * E, 0:S], gate_parts[:].rearrange("p n b e -> p (n b e)"), ident[:]).then_inc(gT_s, 1)

            def expert_bias(g, c):
                if g == 0:
                    pe.wait_ge(be_s, 1)
                pe.wait_ge(gTc_s, g + 1)
                after(pe, start_s, HALF * g + c)
                pe.matmul(R[:], gateT[:], be_r[:, BH * c:BH * (c + 1)].rearrange("p b f -> p (b f)"),
                          start=True, stop=True).then_inc(zb_s, 1)

            for _n in range(WARM_UP):
                pe.transpose(M[0][:, 0, 0:P], ident[:], ident[:])
            for turn in (transpose_c, transpose_v):
                for c in range(HALF):
                    turn(0, c)
            for slot in range(SLOTS):
                g, h = divmod(slot, H)
                if g < G:
                    conv(g, h)
                for at, turn in ((AT_MIX, transpose_mix), (AT_XN, transpose_xn), (AT_V, transpose_v), (AT_C, transpose_c)):
                    for p in due(slot, at):
                        turn(p, 0)
                        turn(p, 1)
                for p in bias_due(slot, AT_SKIP, FIRST_SKIP):
                    sum_heads(p, 0)
                    sum_heads(p, 1)
                for p in due(slot, AT_ROUTE):
                    route(p)
                for p in due(slot, AT_GATES_T):
                    transpose_gates(p)
                for p in due(slot, AT_BIAS0):
                    expert_bias(p, 0)
                for p in due(slot, AT_BIAS1):
                    expert_bias(p, 1)
                for p, u in unit_at(slot):
                    unit(p, u)

        @block.vector
        def _(dve):
            dve.memset(eps[:], EPS).then_inc(eps_s, 1)

            def row_stats(b):
                dve.bn_stats(stats[:, b], x_sb[:, L * b:L * (b + 1)]).then_inc(stats_s, 1)
                dve.wait_ge(stats_s, b + 1)
                dve.bn_aggr(mv[:, b], stats[:, b]).then_inc(mv_s, 1)

            def scales(g, c):
                o = slice(BG * g + BH * c, BG * g + BH * (c + 1))
                dve.wait_ge(sd_s, HALF * g + c + 1)
                dve.reciprocal(rstd[:, o], sd[:, o]).then_inc(rstd_s, 1)
                dve.wait_ge(rstd_s, HALF * g + c + 1)
                dve.scalar_tensor_tensor(out=shift[:, o], in0=mv[:, o, 0], scalar=-1.0, in1=rstd[:, o],
                                         op0=ALU.mult, op1=ALU.mult).then_inc(shift_s, 1)

            def products(g, c):
                dve.wait_ge(ctx_s, 16 * (g + 1))
                dve.wait_ge(v_s, BG * g + BH * (c + 1))
                after(dve, w_hi_s, HALF * (g - 1) + c + 1)
                dve.scalar_tensor_tensor(out=half(w_sb, c), in0=half(v_sb, c), scalar=bias_g[:], in1=half(ctx_sb, c),
                                         op0=ALU.mult, op1=ALU.mult).then_inc(w_s, 1)

            def rest_w(g, c):
                dve.wait_ge(w_hi_s, HALF * g + c + 1)
                if g > 0:
                    dve.wait_ge(turn_s, turn_count(SKIP, g - 1, c))
                dve.tensor_tensor(half(w_lo, c), half(w_sb, c), half(w_hi, c), ALU.subtract).then_inc(w_lo_s, 1)

            def bias_term(g, c):
                dve.wait_ge(turn_s, turn_count(SKIP, g, c))
                after(dve, xt_s, HALF * (g - 1) + c + 1)
                dve.tensor_tensor(half(t_sb, c), T[c][:].rearrange("p n s -> p (n s)"),
                                  half(ctx_sb, c), ALU.mult).then_inc(t_s, 1)

            def weigh(g, h):
                dve.wait_ge(y_s, H * g + h + 1)
                q = h // QH
                if h % QH == 0:
                    after(dve, z4_s, QUADS * g + q - 1)
                ci = cT[:, g % 2, :, :, J * h:J * (h + 1)].rearrange("p n b i -> p (n b) i").unsqueeze(3)
                dve.tensor_tensor(z_sb[:, q % 2, h % QH], Y[(H * g + h) % Y_BANKS][:].rearrange("p n (i j) -> p n i j", i=J),
                                  ci.broadcast_to([P, LB * BG, J, J]), ALU.mult).then_inc(z_s, 1)

            def reduce(g, q):
                dve.wait_ge(z4_s, QUADS * g + q + 1)
                after(dve, mixT_s, QUADS * g + q)
                z = z4[:, q % 2].rearrange("p h n i j -> p (h n) (i j)")
                dve.tensor_tensor(z2[:].rearrange("p h n i j -> p (h n) (i j)"), z[:, :, 0:2 * J], z[:, :, 2 * J:],
                                  ALU.add).then_inc(z2_s, 1)
                dve.wait_ge(z2_s, QUADS * g + q + 1)
                if q == 0 and g > 0:
                    dve.wait_ge(turn_s, turn_count(MIX, g - 1, 1))
                a, b = (z2[:, :, :, i].rearrange("p h n j -> p n h j") for i in range(2))
                dve.tensor_tensor(mixT[:, :, QH * q:QH * (q + 1)], a, b, ALU.add).then_inc(mixT_s, 1)

            def residual(g, c):
                dve.wait_ge(turn_s, turn_count(MIX, g, c))
                dve.wait_ge(xt_s, HALF * g + c + 1)
                after(dve, start_s, HALF * g)
                dve.scalar_tensor_tensor(out=half(x1, c), in0=T[c][:].rearrange("p n s -> p (n s)"),
                                         scalar=g_tanh[:, 0:1], in1=half(xt_sb, c), op0=ALU.mult, op1=ALU.add).then_inc(x1_s, 1)

            def row_stats1(g, c):
                dve.wait_ge(x1_s, HALF * g + c + 1)
                for b in range(BH * c, BH * (c + 1)):
                    dve.bn_stats(stats1[:, b], x1[:, b]).then_inc(stats1_s, 1)
                for b in range(BH * c, BH * (c + 1)):
                    dve.wait_ge(stats1_s, BG * g + b + 1)
                    dve.bn_aggr(mv1[:, b], stats1[:, b]).then_inc(mv1_s, 1)

            def scales1(g, c):
                o = slice(BH * c, BH * (c + 1))
                dve.wait_ge(sd1_s, HALF * g + c + 1)
                after(dve, xn_s, BG * g)
                dve.reciprocal(rstd1[:, o], sd1[:, o]).then_inc(rstd1_s, 1)
                dve.wait_ge(rstd1_s, HALF * g + c + 1)
                dve.scalar_tensor_tensor(out=shift1[:, o], in0=mv1[:, o, 0], scalar=-1.0, in1=rstd1[:, o],
                                         op0=ALU.mult, op1=ALU.mult).then_inc(shift1_s, 1)

            def rest_xn(g, c):
                dve.wait_ge(xhi_s, HALF * g + c + 1)
                o = slice(BH * c, BH * (c + 1))
                dve.tensor_tensor(xnT_lo[:, g % 2, o].rearrange("p b n s -> p (b n) s"), T[c][:],
                                  xnT_hi[:, g % 2, o].rearrange("p b n s -> p (b n) s"), ALU.subtract).then_inc(xlo_s, 1)

            def top_two(g):
                dve.wait_ge(logit_s, g + 1)
                parts = R[:, 0:BG * 2 * E].rearrange("p (b k e) -> p b k e", b=BG, k=2)
                dve.tensor_copy(logits_hi[:], parts[:, :, 0]).then_inc(lhi_s, 1)
                dve.wait_ge(lhi_s, g + 1)
                dve.tensor_tensor(logits[:], parts[:, :, 1], logits_hi[:], ALU.add).then_inc(lcopy_s, 1)
                dve.wait_ge(lcopy_s, g + 1)
                for b in range(BG):
                    dve.max(top8[:, b], logits[:, b]).then_inc(top_s, 1)
                for b in range(BG):
                    dve.wait_ge(top_s, BG * g + b + 1)
                    dve.max_index(idx8[:, b], top8[:, b], logits[:, b]).then_inc(idx_s, 1)
                dve.tensor_tensor(diff[:], top8[:, :, 0], top8[:, :, 1], ALU.subtract).then_inc(diff_s, 1)
                dve.wait_ge(idx_s, BG * (g + 1))
                dve.tensor_copy(idxf[:], idx8[:, :, 0:TOP]).then_inc(idxf_s, 1)

            def gates(g):
                dve.wait_ge(tdiff_s, g + 1)
                for k in range(TOP):
                    dve.tensor_scalar(wts[:, :, k], tdiff[:], g_half[:, k:k + 1], g_half[:, 0:1], ALU.mult, ALU.add).then_inc(wts_s, 1)
                dve.wait_ge(idxf_s, g + 1)
                dve.wait_ge(wts_s, TOP * (g + 1))
                flat = [P, BG * TOP, E]
                dve.tensor_tensor(hit[:], iota_e[:].unsqueeze(1).broadcast_to(flat),
                                  idxf[:].rearrange("p b k -> p (b k)").unsqueeze(2).broadcast_to(flat), ALU.is_equal).then_inc(hit_s, 1)
                dve.wait_ge(hit_s, g + 1)
                dve.tensor_tensor(gk[:].rearrange("p b k e -> p (b k) e"), hit[:],
                                  wts[:].rearrange("p b k -> p (b k)").unsqueeze(2).broadcast_to(flat), ALU.mult).then_inc(gk_s, 1)
                dve.wait_ge(gk_s, g + 1)
                after(dve, add_s, UNITS * (g - 1))
                dve.tensor_tensor(gate[:, g % 2], gk[:, :, 0], gk[:, :, 1], ALU.add).then_inc(gate_s, 1)
                dve.wait_ge(gate_s, g + 1)
                dve.tensor_copy(gate_r[:], gate[:, g % 2]).then_inc(gate_r_s, 1)
                dve.wait_ge(gate_r_s, g + 1)
                after(dve, gT_s, g)
                dve.tensor_copy(gate_parts[:, 0:2].rearrange("p n b e -> p n (b e)"),
                                gate_r[:].bitcast(F32).rearrange("p b e -> p (b e)").unsqueeze(1).broadcast_to([P, 2, BG * E])).then_inc(gate_p_s, 1)
                dve.tensor_tensor(gate_parts[:, 2], gate[:, g % 2], gate_r[:].bitcast(F32), ALU.subtract).then_inc(gate_p_s, 1)

            def start(g, c):
                if g == 0:
                    dve.wait_ge(we_lo_s, WCH)
                dve.wait_ge(zb_s, HALF * g + c + 1)
                for b in range(BH * c, BH * (c + 1)):
                    after(dve, out_s[g % 2][b], 16 * (g // 2))
                dve.tensor_tensor(half(acc[:, g % 2], c), R[:], half(x1, c), ALU.add).then_inc(start_s, 1)

            def add(g, u):
                b, e = u // (E // 2), 2 * (u % (E // 2))
                m = unit_psum(UNITS * g + u)
                dve.wait_ge(m_s, UNITS * g + u + 1)
                dve.wait_ge(start_s, HALF * g + u // (UNITS // HALF) + 1)
                after(dve, add_s, UNITS * g + u)
                dve.scalar_tensor_tensor(out=acc[:, g % 2, b], in0=m[:, 0], scalar=gate[:, g % 2, b, e:e + 1], in1=acc[:, g % 2, b],
                                         op0=ALU.mult, op1=ALU.add).then_inc(acc_s, 1)
                dve.wait_ge(acc_s, UNITS * g + u + 1)
                dve.scalar_tensor_tensor(out=acc[:, g % 2, b], in0=m[:, 1], scalar=gate[:, g % 2, b, e + 1:e + 2], in1=acc[:, g % 2, b],
                                         op0=ALU.mult, op1=ALU.add).then_inc(add_s, 1)

            for c in range(HALF):
                dve.wait_ge(x_half_in[c], 16)
                for b in range(BH * c, BH * (c + 1)):
                    row_stats(b)
            scales(0, 0)
            scales(0, 1)
            for c in range(HALF):
                dve.wait_ge(turn_s, turn_count(C, 0, c))
                dve.tensor_copy(cT[:, 0, :, BH * c:BH * (c + 1), :], T[c][:].rearrange("p (n b) s -> p n b s", n=LB)).then_inc(cT_s, 1)
            pairs(dve, 0, 0).then_inc(first_kv_s, 1)
            dve.wait_ge(tanh_s, 1)
            dve.tensor_tensor(bias_g[:], bias_sb[:], g_tanh[:, 0:1], ALU.mult).then_inc(gains_s, 1)
            for k, sign in enumerate((0.5, -0.5)):
                dve.tensor_scalar(g_half[:, k:k + 1], g_tanh[:, 1:2], sign, None, ALU.mult).then_inc(gains_s, 1)
            dve.wait_ge(gains_s, 3)
            for c in range(HALF):
                products(0, c)
            dve.wait_ge(ones_s, 1)
            dve.tensor_copy(head_ones_r[:], head_ones[:]).then_inc(ones_r_s, 1)
            for slot in range(SLOTS):
                g, h = divmod(slot, H)
                if g < G:
                    weigh(g, h)
                for b in range(BG):
                    for p in due(slot, AT_STATS, b):
                        if b == 0:
                            dve.wait_ge(x_in[p], 16)
                        row_stats(BG * p + b)
                for q in range(QUADS):
                    for p in due(slot, (QH * q, 0), REDUCE_LATER):
                        reduce(p, q)
                for c in range(HALF):
                    for p in due(slot, AT_RESIDUAL):
                        residual(p, c)
                    for p in due(slot, AT_RESIDUAL, c):
                        row_stats1(p, c)
                    for p in due(slot, AT_NORM1):
                        scales1(p, c)
                for p in due(slot, AT_SCALES):
                    scales(p, 0)
                    scales(p, 1)
                for c in range(HALF):
                    for p in due(slot, AT_REST):
                        rest_xn(p, c)
                    for p in due(slot, AT_PRODUCTS, c):
                        products(p, c)
                    for p in bias_due(slot, AT_WREST, FIRST_WREST, c):
                        rest_w(p, c)
                    for p in bias_due(slot, AT_TERM, FIRST_TERM, c):
                        bias_term(p, c)
                for p in due(slot, AT_TOP):
                    top_two(p)
                for p in due(slot, AT_GATES):
                    gates(p)
                for p in due(slot, AT_START0):
                    start(p, 0)
                for p in due(slot, AT_START1):
                    start(p, 1)
                for p, u in unit_at(slot):
                    add(p, u)
                if slot in range(WE_REST, WE_REST + 2 * WCH, 2):
                    n = (slot - WE_REST) // 2
                    dve.wait_ge(we_hi_s, n + 1)
                    dve.tensor_tensor(piece(we_lo, n), piece(we_f, n), piece(we_hi, n), ALU.subtract).then_inc(we_lo_s, 1)
                if slot == WE_REST + 2 * WCH:
                    dve.wait_ge(wr_hi_s, 1)
                    dve.tensor_tensor(wr_parts[:, :, 1], wr_f[:], wr_parts[:, :, 0], ALU.subtract).then_inc(wr_lo_s, 1)
                    rest = slice(BG * E, 2 * BG * E)
                    dve.wait_ge(be_hi_s, 1)
                    dve.tensor_tensor(be_r[rest], be_f[rest], be_r[rest].bitcast(F32), ALU.subtract).then_inc(be_s, 1)
                    dve.wait_ge(iota_s, 1)


def kernel(x, fside_S2_0, ctx_2048, g_xattn, g_ffn, L0_xattn_k, L0_ffn_Wr, L0_ffn_We, L0_ffn_be):
    import numpy as np
    import concourse.bacc as bacc
    from concourse.bass_utils import run_bass_kernel_spmd

    kpad = np.zeros((H, KPAD), np.float32)
    kpad[:, P:] = np.asarray(L0_xattn_k)
    toep = np.lib.stride_tricks.sliding_window_view(kpad, L, axis=1)[:, P:0:-1].transpose(1, 0, 2)
    arrays = {"x": x, "bias": fside_S2_0, "ctx": ctx_2048, "g_xattn": g_xattn, "g_ffn": g_ffn, "toep": toep,
              "wr": L0_ffn_Wr, "we": L0_ffn_We, "be": L0_ffn_be}
    arrays = {f"in_{n}": np.ascontiguousarray(a) for n, a in arrays.items()}
    nc = bacc.Bacc("TRN2", target_bir_lowering=False, num_devices=1)
    args = [nc.dram_tensor(n, a.shape, mybir.dt.from_np(a.dtype), kind="ExternalInput").ap() for n, a in arrays.items()]
    out = nc.dram_tensor("out_0", (B, S, F), F32, kind="ExternalOutput").ap()
    build(nc, *args, out)
    r = run_bass_kernel_spmd(nc, [arrays], core_ids=[0])
    return r.results[0]["out_0"]
```
